# Optimizing a Trainium2 kernel written in Bass

```python
import numpy as np
import jax
import jax.numpy as jnp

def _softmax(x, axis=-1):
    return jax.nn.softmax(x, axis=axis)

def _gelu(x):
    return jax.nn.gelu(x, approximate=True)

def _silu(x):
    return jax.nn.silu(x)

def _sigmoid(x):
    return jax.nn.sigmoid(x)

def _layernorm(x, axis=-1, eps=1e-05):
    m = jnp.mean(x, axis=axis, keepdims=True)
    v = jnp.var(x, axis=axis, keepdims=True)
    return (x - m) / jnp.sqrt(v + eps)

def _scatter_add(tgt, idx, src, axis=0):
    return tgt.at[idx].add(src)

def _segment_sum(src, seg, n):
    return jax.ops.segment_sum(src, seg, n)
kernel_name = 'mk_gnn_preln_d4_gnn_r64_8a1e35'

def setup_inputs(seed: int=0):
    np.random.seed(seed)
    _w = jnp.asarray

    def _rec_inputs():
        import jax
        import jax.numpy as jnp
        _gk = jax.random.key(seed)
        x = -0.0003713 + 1 * jax.random.normal(jax.random.fold_in(_gk, 1), (100000, 128), jnp.float32)
        src = jax.random.randint(jax.random.fold_in(_gk, 2), (25000,), 0, 100000, jnp.int32)
        dst = jax.random.randint(jax.random.fold_in(_gk, 3), (25000,), 0, 100000, jnp.int32)
        _o = jnp.argsort(dst, stable=True)
        src = src[_o]
        dst = dst[_o]
        edge_weight = jax.random.uniform(jax.random.fold_in(_gk, 14), (25000,), jnp.float32, 0.0, 0.999999)
        return (x, src, dst, edge_weight)
    x, src, dst, edge_weight = _rec_inputs()

    def _L0_gnn_setup():
        import jax, jax.numpy as jnp
        import numpy as np
        N = 100000
        E = 25000
        D_IN = 128
        D_OUT = 128
        key = jax.random.key(seed)
        k1, k2, k3, k4 = jax.random.split(key, 4)
        H = jax.random.normal(k1, (N, D_IN), dtype=jnp.float32)
        src = jax.random.randint(k2, (E,), 0, N, dtype=jnp.int32)
        dst = jax.random.randint(k3, (E,), 0, N, dtype=jnp.int32)
        W = jax.random.normal(k4, (D_OUT, 2 * D_IN), dtype=jnp.float32) * 0.05
        b = jnp.zeros((D_OUT,), dtype=jnp.float32)
        return {'H': H, 'src': src, 'dst': dst, 'W': W, 'b': b}
    _L0_gnn_all = _L0_gnn_setup()
    _L0_gnn_in = {k: v for k, v in _L0_gnn_all.items() if k in ('W', 'b')}
    del _L0_gnn_all

    def _L1_gnn_setup():
        import jax, jax.numpy as jnp
        import numpy as np
        BN_EPS = 1e-05

        def _batchnorm(h, gamma, beta):
            mean = jnp.mean(h, axis=0)
            var = jnp.var(h, axis=0)
            return (h - mean) * jax.lax.rsqrt(var + BN_EPS) * gamma + beta
        N, E, D_IN, D_OUT = (50000, 12500, 128, 128)
        key = jax.random.key(seed)
        ks = jax.random.split(key, 6)
        x = jax.random.normal(ks[0], (N, D_IN), dtype=jnp.float32)
        edge_index = jax.random.randint(ks[1], (2, E), 0, N, dtype=jnp.int32)
        lim1 = 1.0 / np.sqrt(2 * D_IN)
        lim2 = 1.0 / np.sqrt(D_OUT)
        W1 = jax.random.uniform(ks[2], (D_OUT, 2 * D_IN), jnp.float32, -lim1, lim1)
        b1 = jax.random.uniform(ks[3], (D_OUT,), jnp.float32, -lim1, lim1)
        W2 = jax.random.uniform(ks[4], (D_OUT, D_OUT), jnp.float32, -lim2, lim2)
        b2 = jax.random.uniform(ks[5], (D_OUT,), jnp.float32, -lim2, lim2)
        g1 = jnp.ones((D_OUT,), jnp.float32)
        be1 = jnp.zeros((D_OUT,), jnp.float32)
        g2 = jnp.ones((D_OUT,), jnp.float32)
        be2 = jnp.zeros((D_OUT,), jnp.float32)
        return {'x': x, 'edge_index': edge_index, 'W1': W1, 'b1': b1, 'g1': g1, 'be1': be1, 'W2': W2, 'b2': b2, 'g2': g2, 'be2': be2}
    _L1_gnn_all = _L1_gnn_setup()
    _L1_gnn_in = {k: v for k, v in _L1_gnn_all.items() if k in ('W1', 'b1', 'g1', 'be1', 'W2', 'b2', 'g2', 'be2')}
    del _L1_gnn_all

    def _L2_gnn_setup():
        import jax, jax.numpy as jnp
        import numpy as np
        N = 100000
        E = 15625
        D_IN = 128
        D_OUT = 128
        key = jax.random.key(seed)
        ks = jax.random.split(key, 6)
        ego_embedding = jax.random.normal(ks[0], (N, D_IN), dtype=jnp.float32)
        norm = jax.random.uniform(ks[1], (N, 1), dtype=jnp.float32)
        src = jax.random.randint(ks[2], (E,), 0, N, dtype=jnp.int32)
        dst = jax.random.randint(ks[3], (E,), 0, N, dtype=jnp.int32)
        s = 1.0 / np.sqrt(D_IN)
        W1 = jax.random.uniform(ks[4], (D_IN, D_OUT), dtype=jnp.float32, minval=-s, maxval=s)
        W2 = jax.random.uniform(ks[5], (D_IN, D_OUT), dtype=jnp.float32, minval=-s, maxval=s)
        return {'ego_embedding': ego_embedding, 'norm': norm, 'src': src, 'dst': dst, 'W1': W1, 'W2': W2}
    _L2_gnn_all = _L2_gnn_setup()
    _L2_gnn_in = {k: v for k, v in _L2_gnn_all.items() if k in ('W1', 'W2')}
    del _L2_gnn_all

    def _L3_gnn_setup():
        import jax, jax.numpy as jnp
        import numpy as np
        N_NODES = 50000
        N_EDGES = 12500
        D = 128
        key = jax.random.key(seed)
        ks = jax.random.split(key, 8)
        x = jax.random.normal(ks[0], (N_NODES, D), dtype=jnp.float32)
        src = jax.random.randint(ks[1], (N_EDGES,), 0, N_NODES, dtype=jnp.int64)
        dst = jax.random.randint(ks[2], (N_EDGES,), 0, N_NODES, dtype=jnp.int64)
        edge_weights = jax.random.uniform(ks[3], (N_EDGES,), dtype=jnp.float32)
        scale = 1.0 / np.sqrt(D)
        W1 = jax.random.normal(ks[4], (D, D), dtype=jnp.float32) * scale
        b1 = jnp.zeros((D,), dtype=jnp.float32)
        W2 = jax.random.normal(ks[5], (D, D), dtype=jnp.float32) * scale
        b2 = jnp.zeros((D,), dtype=jnp.float32)
        return {'x': x, 'src': src, 'dst': dst, 'edge_weights': edge_weights, 'W1': W1, 'b1': b1, 'W2': W2, 'b2': b2}
    _L3_gnn_all = _L3_gnn_setup()
    _L3_gnn_in = {k: v for k, v in _L3_gnn_all.items() if k in ('W1', 'b1', 'W2', 'b2')}
    del _L3_gnn_all
    return {'x': x, 'src': src, 'dst': dst, 'edge_weight': edge_weight, 'L0_gnn_W': _L0_gnn_in['W'], 'L0_gnn_b': _L0_gnn_in['b'], 'L1_gnn_W1': _L1_gnn_in['W1'], 'L1_gnn_b1': _L1_gnn_in['b1'], 'L1_gnn_g1': _L1_gnn_in['g1'], 'L1_gnn_be1': _L1_gnn_in['be1'], 'L1_gnn_W2': _L1_gnn_in['W2'], 'L1_gnn_b2': _L1_gnn_in['b2'], 'L1_gnn_g2': _L1_gnn_in['g2'], 'L1_gnn_be2': _L1_gnn_in['be2'], 'L2_gnn_W1': _L2_gnn_in['W1'], 'L2_gnn_W2': _L2_gnn_in['W2'], 'L3_gnn_W1': _L3_gnn_in['W1'], 'L3_gnn_b1': _L3_gnn_in['b1'], 'L3_gnn_W2': _L3_gnn_in['W2'], 'L3_gnn_b2': _L3_gnn_in['b2']}

def reference(x, src, dst, edge_weight, L0_gnn_W, L0_gnn_b, L1_gnn_W1, L1_gnn_b1, L1_gnn_g1, L1_gnn_be1, L1_gnn_W2, L1_gnn_b2, L1_gnn_g2, L1_gnn_be2, L2_gnn_W1, L2_gnn_W2, L3_gnn_W1, L3_gnn_b1, L3_gnn_W2, L3_gnn_b2):
    import jax
    import jax.numpy as jnp

    def _L0_gnn_ref(H, src, dst, W, b):
        import jax, jax.numpy as jnp
        import numpy as np
        N = 100000
        E = 25000
        D_IN = 128
        D_OUT = 128
        gathered = H[dst]
        agg = jax.ops.segment_max(gathered, src, num_segments=N)
        deg = jax.ops.segment_sum(jnp.ones((src.shape[0],), jnp.float32), src, num_segments=N)
        H_neigh = jnp.where(deg[:, None] > 0, agg, 0.0)
        H_concat = jnp.concatenate([H, H_neigh], axis=1)
        return H_concat @ W.T + b

    def _L1_gnn_ref(x, edge_index, W1, b1, g1, be1, W2, b2, g2, be2):
        import jax, jax.numpy as jnp
        import numpy as np
        BN_EPS = 1e-05

        def _batchnorm(h, gamma, beta):
            mean = jnp.mean(h, axis=0)
            var = jnp.var(h, axis=0)
            return (h - mean) * jax.lax.rsqrt(var + BN_EPS) * gamma + beta
        src, dst = (edge_index[0], edge_index[1])
        edge_features = jnp.concatenate([x[src], x[dst]], axis=1)
        h = edge_features @ W1.T + b1
        h = jax.nn.relu(_batchnorm(h, g1, be1))
        h = h @ W2.T + b2
        edge_updates = jax.nn.relu(_batchnorm(h, g2, be2))
        x_out = jax.ops.segment_sum(edge_updates, dst, num_segments=x.shape[0])
        return x_out

    def _L2_gnn_ref(ego_embedding, norm, src, dst, W1, W2):
        import jax, jax.numpy as jnp
        import numpy as np
        N = 100000
        E = 15625
        D_IN = 128
        D_OUT = 128
        h_src = ego_embedding[src]
        h_dst = ego_embedding[dst]
        msg = h_src @ W1 + h_src * h_dst @ W2
        msg = msg * (norm[src] * norm[dst])
        h_N = jax.ops.segment_sum(msg, dst, num_segments=N)
        h_N = h_N + ego_embedding @ W1
        h = jnp.where(h_N >= 0, h_N, 0.2 * h_N)
        nrm = jnp.sqrt(jnp.sum(h * h, axis=1, keepdims=True))
        h = h / jnp.maximum(nrm, 1e-12)
        return h

    def _L3_gnn_ref(x, src, dst, edge_weights, W1, b1, W2, b2):
        import jax, jax.numpy as jnp
        import numpy as np
        N_NODES = 50000
        N_EDGES = 12500
        D = 128
        n_nodes = x.shape[0]
        deg = jax.ops.segment_sum(jnp.ones_like(src, dtype=x.dtype), src, num_segments=n_nodes)
        deg = jnp.maximum(deg, 1.0)
        coef = jax.lax.rsqrt(deg[src] * deg[dst]) * edge_weights
        msgs = x[src] * coef[:, None]
        agg = jax.ops.segment_sum(msgs, dst, num_segments=n_nodes)
        h = jax.nn.relu(agg @ W1 + b1)
        return h @ W2 + b2
    edge_index = jnp.stack([src, dst])
    deg = jnp.maximum(jax.ops.segment_sum(jnp.ones(dst.shape, jnp.float32), dst, num_segments=100000), 1.0)
    deg_isqrt = deg ** (-0.5)
    h = jnp.maximum(_layernorm(x, axis=-1), 0.0)
    x = x + _L0_gnn_ref(h, src, dst, L0_gnn_W, L0_gnn_b)
    h = jnp.maximum(_layernorm(x, axis=-1), 0.0)
    x = x + _L1_gnn_ref(h, edge_index, L1_gnn_W1, L1_gnn_b1, L1_gnn_g1, L1_gnn_be1, L1_gnn_W2, L1_gnn_b2, L1_gnn_g2, L1_gnn_be2)
    h = jnp.maximum(_layernorm(x, axis=-1), 0.0)
    x = x + _L2_gnn_ref(h, deg_isqrt[:, None], src, dst, L2_gnn_W1, L2_gnn_W2)
    h = jnp.maximum(_layernorm(x, axis=-1), 0.0)
    x = x + _L3_gnn_ref(h, src, dst, edge_weight, L3_gnn_W1, L3_gnn_b1, L3_gnn_W2, L3_gnn_b2)
    return x

_drawn_inputs = setup_inputs


def setup_inputs(seed=0):
    import zlib

    import numpy as np

    out = dict(_drawn_inputs(seed))
    spreads = {'L0_gnn_b': (0.0, 0.1),
     'L1_gnn_g1': (1.0, 0.2),
     'L1_gnn_be1': (0.0, 0.309),
     'L1_gnn_g2': (1.0, 0.2),
     'L1_gnn_be2': (0.0, 0.1),
     'L3_gnn_b1': (0.0, 0.1),
     'L3_gnn_b2': (0.0, 0.1)}
    factors = {'L1_gnn_b1': 8.0, 'L1_gnn_b2': 8.0, 'L2_gnn_W2': 4.125}
    for name, (base, spread) in spreads.items():
        noise = np.random.default_rng([zlib.crc32(name.encode()), seed]).standard_normal(out[name].shape)
        drawn = base * np.exp(spread * noise) if base else spread * noise
        out[name] = jnp.asarray(drawn.astype(out[name].dtype))
    for name, factor in factors.items():
        out[name] = (out[name] * factor).astype(out[name].dtype)
    return out
```

```python
from contextlib import ExitStack

import concourse.bass as bass
from concourse import mybir

F32 = mybir.dt.float32
I32 = mybir.dt.int32
BF16 = mybir.dt.bfloat16
ALU = mybir.AluOpType
ACT = mybir.ActivationFunctionType

P = 128
G = 4
ROW = G * P
XW = P + 2
LN_EPS = 1e-05
BN_EPS = 1e-05
SORT = 2 * P * P
IDX_BITS = 15
FAR = 1 << 20


class Turn:

    def __init__(self, group, off, last, unroll):
        self.group, self.off, self.last, self.unroll = group, off, last, unroll
        self.fixed = isinstance(group, int)
        self.n = group * unroll + off

    def slot(self, ring):
        return self.off % ring

    def round(self, ring):
        return self.group * (self.unroll // ring) + self.off // ring

    def past(self, steps):
        return not self.fixed or self.n >= steps


def run_steps(eng, count, stages, unroll=4):
    reach = max(lag + (more[0] if more else 4) for lag, _, *more in stages)
    stages = [(lag, stage) for lag, stage, *_ in stages]
    most = max(lag for lag, _ in stages)
    first = -(-reach // unroll)
    last = max((count - 1) // unroll, first)

    def peeled(n):
        for lag, stage in stages:
            if 0 <= n - lag < count:
                stage(Turn(0, n - lag, n - lag == count - 1, unroll))

    for n in range(first * unroll if last > first else 0):
        peeled(n)
    if last > first:
        with eng.Fori(first, last) as group:
            for u in range(unroll):
                for lag, stage in stages:
                    stage(Turn(group, u - lag, False, unroll))
    for n in range(last * unroll if last > first else 0, count + most):
        peeled(n)


def build_gnn(nc, x, src, dst, edge_weight, wself_t, wneigh_t, bias0, e1_src_t, e1_dst_t, e1_b, e1_g, e1_be,
              e2_t, e2_b, e2_g, e2_be, m1, m2, c1, c1_b, c2, c2_b, out):
    N = x.shape[0]
    E = src.shape[0]
    CHUNKS = -(-E // ROW)
    TILES = G * CHUNKS
    TAIL = E - (CHUNKS - 1) * ROW
    BLOCKS = -(-N // ROW)
    REST = (N - (BLOCKS - 1) * ROW) // G
    HALF = N // 2
    LIFT = (1 << 16) - HALF
    PAD_KEY = (1 << 16) + 60000 - 256 - LIFT
    assert (N - (BLOCKS - 1) * ROW) % G == 0 and HALF + 256 < 60000 and PAD_KEY >= N and E <= 1 << IDX_BITS

    def dram(name, shape, dt=F32):
        return nc.dram_tensor(name, shape, dt, kind="Internal").ap()

    state = dram("state", (N + TILES * P, XW))
    state3 = dram("state3", (N, P))
    dst_rows = dram("dst_rows", (CHUNKS, P, G * P))
    key_line = dram("key_line", (2, SORT + 2))
    mask_line = dram("mask_line", (2, SORT), BF16)
    start_line = dram("start_line", (2, 2 * P + 1))
    before_line = dram("before_line", (2, 2 * P))
    payload = dram("payload", (E, 4))

    x_blocks = x.rearrange("(a g) d -> a (g d)", g=G)
    state_blocks = state.rearrange("(a g) d -> a (g d)", g=G)
    state3_blocks = state3.rearrange("(a g) d -> a (g d)", g=G)
    out_blocks = out.rearrange("(a g) d -> a (g d)", g=G)

    with ExitStack() as ctx:
        def sb(name, shape, dt=F32):
            return ctx.enter_context(nc.sbuf_tensor(name, shape, dt))

        def sem(name):
            return ctx.enter_context(nc.semaphore(name))

        def sems(name, n):
            return [sem(f"{name}{i}") for i in range(n)]

        banks = [ctx.enter_context(nc.psum_tensor(f"bank{i}", [P, ROW], F32)) for i in range(8)]

        W = {n: sb(n, [P, P]) for n in ("wself", "wneigh", "e1s", "e1d", "e2", "m1w", "m2w", "c1w", "c2w")}
        cols = sb("cols", [P, 8])
        E1B, E1G, E1BE, E2B, E2G, E2BE, C1B = range(7)
        bias_rows = sb("bias_rows", [1, 2, ROW])
        ident = sb("ident", [P, P])
        ones_row = sb("ones_row", [1, P])
        eps_col = sb("eps_col", [P, 1])
        zero_rows = sb("zero_rows", [P, G * XW])
        relu_b = sb("relu_b", [P, P])
        quiet = sb("quiet", [P, ROW])

        hidden = sb("hidden", [P, max(CHUNKS * ROW, 17 * ROW)])
        views = [0]

        def early(dt=F32, halves=2):
            at = views[0]
            views[0] += halves * 2 * P
            view = hidden[:, at:at + halves * 2 * P]
            view = view.bitcast(dt) if dt != F32 else view
            return view.rearrange("p (s f) -> p s f", s=2) if halves == 2 else view

        keys = early(I32)
        weights_in = early(halves=1)
        sort_a = early()
        sort_b = early()
        place = early(I32, 1)
        place_f = early(halves=1)
        gray = early(I32, 1)
        flip = early(I32, 1)
        tmp_i = early(I32)
        tmp_f = early()
        key_f = early()
        idx_f = early()
        prev_f = early()
        next_f = early()
        end_f = early()
        count_f = early()
        first_f = early()
        pack = early(halves=4).rearrange("p (f w) -> p f w", w=4)
        mask_b = sb("mask_b", [P, 2, 2 * P], BF16)
        row_max = sb("row_max", [P, 2, 2])
        row_before = sb("row_before", [P, 2, 2])
        line = sb("line", [2, 2 * P])
        line2 = sb("line2", [2, 2 * P])
        minus1 = sb("minus1", [2, 1])
        zero2 = sb("zero2", [2, 1])
        idx_t = sb("idx_t", [P, 2, 2 * P], I32)
        end_t = sb("end_t", [P, 2, 2 * P], I32)
        count_t = sb("count_t", [P, 2, 2 * P])
        pay = sb("pay", [P, 2, TILES, 4])
        dst_s_t = sb("dst_s_t", [P, TILES], I32)
        src_t = sb("src_t", [P, TILES], I32)
        dst_t = sb("dst_t", [P, TILES], I32)
        norm_t = sb("norm_t", [P, TILES])
        coef_t = sb("coef_t", [P, TILES])
        deg_s_t = sb("deg_s_t", [P, TILES])
        deg_d_t = sb("deg_d_t", [P, TILES])

        rows_ab = sb("rows_ab", [P, 8, G, XW])
        rows_a, rows_b = rows_ab[:, 0:4], rows_ab[:, 4:8]
        rows_o = sb("rows_o", [P, 4, G, XW])
        mask = sb("mask", [P, 4, ROW], BF16)
        index = sb("index", [P, 4, 2, G], I32)
        facts = sb("facts", [P, 4, 2, G])
        feat_a = sb("feat_a", [P, 2, ROW])
        feat_b = sb("feat_b", [P, 2, ROW])
        feat_cd = sb("feat_cd", [P, 4, ROW])
        feat_c, feat_d = feat_cd[:, 0:2], feat_cd[:, 2:4]
        bn_parts = sb("bn_parts", [P, CHUNKS, 6])
        bn_mv = sb("bn_mv", [P, 2])
        bn_sd = sb("bn_sd", [P, 1])
        bn_scale = sb("bn_scale", [P, 1])
        bn_tmp = sb("bn_tmp", [P, 1])
        bn_shift = sb("bn_shift", [P, 1])

        PHASES = ["index", "dense1", "layer0", "dense2", "layer1a", "layer1b", "layer1c", "layer2", "layer3"]
        engines_done = sem("engines_done")

        def phase_end(eng, name):
            at = PHASES.index(name) + 1
            eng.drain().then_inc(engines_done, 1)
            eng.wait_ge(engines_done, 5 * at)
            eng.nop(nofuse=True)

        class RowNorm:

            def __init__(self, name, banks2, phases):
                self.tile = sb(name + "_h", [P, 2, G, P])
                self.stat = sb(name + "_stat", [P, 2, G, 6])
                self.small = sb(name + "_small", [P, 2, 8, G])
                self.banks = banks2
                self.phases = phases
                self.chain, self.var, self.rooted, self.inverse, self.scaled, self.rows, self.turned = (
                    sem(f"{name}_{k}") for k in ("chain", "var", "root", "inverse", "scaled", "rows", "turned"))

            def begin(self, phase):
                self.base = self.chain_base = 0
                for name, steps, self.links in self.phases:
                    if name == phase:
                        return self
                    self.base += steps
                    self.chain_base += steps * self.links
                raise KeyError(phase)

            def stats(self, v, t, rows, parts=P, degree=None):
                s = t.slot(2)
                st = self.stat[0:parts, s]
                total, diff, q, d2, var = (self.small[0:parts, s, i] for i in range(5))
                for g in range(G):
                    last = v.bn_stats(st[:, g, :], rows[0:parts, g, 0:P])
                last.then_inc(self.chain, 1)
                v.wait_ge(self.chain, self.chain_base + t.n * self.links + 1)
                v.tensor_tensor(total, st[:, :, 1], st[:, :, 4], ALU.add)
                v.tensor_tensor(diff, st[:, :, 1], st[:, :, 4], ALU.subtract)
                v.tensor_tensor(q, st[:, :, 2], st[:, :, 5], ALU.add).then_inc(self.chain, 1)
                v.wait_ge(self.chain, self.chain_base + t.n * self.links + 2)
                v.scalar_tensor_tensor(d2, diff, P / 4.0, diff, ALU.mult, ALU.mult).then_inc(self.chain, 1)
                v.wait_ge(self.chain, self.chain_base + t.n * self.links + 3)
                if degree is None:
                    v.tensor_tensor(var, q, d2, ALU.add).then_inc(self.var, 1)
                    return
                v.tensor_tensor(d2, q, d2, ALU.add).then_inc(self.chain, 1)
                v.wait_ge(self.chain, self.chain_base + t.n * self.links + 4)
                v.tensor_scalar(d2, d2, 1.0 / P, LN_EPS, ALU.mult, ALU.add).then_inc(self.chain, 1)
                v.wait_ge(self.chain, self.chain_base + t.n * self.links + 5)
                v.scalar_tensor_tensor(var, degree, 1.0, d2, ALU.max, ALU.mult).then_inc(self.var, 1)

            def root(self, a, t, parts=P, degree=False):
                s = t.slot(2)
                a.wait_ge(self.var, self.base + t.n + 1)
                if degree:
                    nc.scalar.activation(self.small[0:parts, s, 7], self.small[0:parts, s, 4],
                                         ACT.Sqrt).then_inc(self.rooted, 1)
                else:
                    nc.scalar.activation(self.small[0:parts, s, 7], self.small[0:parts, s, 4], ACT.Sqrt,
                                         bias=eps_col[0:parts, 0:1], scale=1.0 / P).then_inc(self.rooted, 1)

            def scale(self, v, t, parts=P):
                s = t.slot(2)
                rstd, shift = self.small[0:parts, s, 5], self.small[0:parts, s, 6]
                v.wait_ge(self.rooted, self.base + t.n + 1)
                v.reciprocal(rstd, self.small[0:parts, s, 7]).then_inc(self.inverse, 1)
                v.wait_ge(self.inverse, self.base + t.n + 1)
                v.scalar_tensor_tensor(shift, self.small[0:parts, s, 0], -0.5, rstd,
                                       ALU.mult, ALU.mult).then_inc(self.scaled, 1)

            def relu(self, a, t, rows, parts=P):
                s = t.slot(2)
                a.wait_ge(self.scaled, self.base + t.n + 1)
                if t.past(2):
                    a.wait_ge(self.turned, self.base + t.n - 1)
                for g in range(G):
                    last = nc.scalar.activation(self.tile[0:parts, s, g, :], rows[0:parts, g, 0:P], ACT.Relu,
                                                bias=self.small[0:parts, s, 6, g:g + 1],
                                                scale=self.small[0:parts, s, 5, g:g + 1])
                last.then_inc(self.rows, 1)

            def turn(self, p, t, taken, parts=P, ready=None):
                s = t.slot(2)
                if ready is None:
                    p.wait_ge(self.rows, self.base + t.n + 1)
                else:
                    p.wait_ge(ready.sem, ready.base + t.n + 1)
                if t.past(2):
                    p.wait_ge(taken.sem, taken.base + t.n - 1)
                for g in range(G):
                    last = nc.tensor.transpose(self.banks[s][:, g * P:g * P + parts],
                                               self.tile[0:parts, s, g, :], ident[0:parts, 0:parts])
                last.then_inc(self.turned, 1)

        norm_a = RowNorm("na", banks[0:2], [("d1", BLOCKS, 3), ("l0", CHUNKS, 3), ("d2", BLOCKS, 3), ("l1", CHUNKS, 3),
                                            ("l2", CHUNKS, 5), ("l3", CHUNKS, 3)])
        norm_b = RowNorm("nb", banks[2:4], [("l1", CHUNKS, 3), ("l2", CHUNKS, 3)])

        class Count:

            def __init__(self, semaphore, base):
                self.sem, self.base = semaphore, base

        def in_turn(name, *steps):
            shared, base, views = sem(name), 0, []
            for n in steps:
                views.append(Count(shared, base))
                base += n
            return views

        (d1_copied, l0_mm, d2_copied, l1_copied, l1b_act, l1c_act, l2_copied, l3_mm1) = in_turn("d1_copied_and_later", BLOCKS, CHUNKS, BLOCKS, CHUNKS, CHUNKS, CHUNKS, CHUNKS, CHUNKS)
        (d1_mm, l0_ready, d2_mm, l1_mm, l1b_mm, l1c_turned, l2_mm, l3_mm2) = in_turn("d1_mm_and_later", BLOCKS, CHUNKS, BLOCKS, CHUNKS, CHUNKS, CHUNKS, CHUNKS, CHUNKS)
        (d1_ready, l0_staged, d2_leaky, l1_hidden, l1b_hidden, l1c_ready, l2_ready, l3_ready) = in_turn("d1_ready_and_later", BLOCKS, CHUNKS, BLOCKS, CHUNKS, CHUNKS, CHUNKS, CHUNKS, CHUNKS)
        (l0_staged2, d2_norm, l1_degs, l1c_staged, l2_staged, l3_staged) = in_turn("l0_staged2_and_later", CHUNKS, BLOCKS, CHUNKS, CHUNKS, CHUNKS, CHUNKS)
        (l0_counts, d2_root, l1_staged, l1c_facts, l2_staged2, l3_staged2) = in_turn("l0_counts_and_later", CHUNKS, BLOCKS, CHUNKS, CHUNKS, CHUNKS, CHUNKS)
        (d2_inv, l1_staged_d, l1c_facts2, l2_facts, l3_facts) = in_turn("d2_inv_and_later", BLOCKS, CHUNKS, CHUNKS, CHUNKS, CHUNKS)
        (scanned0, d2_x3, scanned1, scanned2, scanned3) = in_turn("scanned0_and_later", CHUNKS, BLOCKS, CHUNKS, CHUNKS, CHUNKS)
        (d2_ready, l2_prod, l3_coef) = in_turn("d2_ready_and_later", BLOCKS, CHUNKS, CHUNKS)
        (d2_chain, l2_chain, l3_act) = in_turn("d2_chain_and_later", BLOCKS, 2 * CHUNKS, CHUNKS)
        (d2_fifth, l2_scaled) = in_turn("d2_fifth_and_later", BLOCKS, CHUNKS)
        (l2_sum,) = in_turn("l2_sum_and_later", CHUNKS)
        (l2_leaky,) = in_turn("l2_leaky_and_later", CHUNKS)
        (l2_norm,) = in_turn("l2_norm_and_later", CHUNKS)
        (l2_root,) = in_turn("l2_root_and_later", CHUNKS)

        class Ring:

            def __init__(self, slots, per_step, phase):
                self.slots, self.per_step, self.phase = slots, per_step, phase

            def __getitem__(self, slot):
                return self.slots[slot]

            def base(self, slot):
                return self.phase * self.per_step * len(range(slot, CHUNKS, 4))

        gathered_a, stored, rows_back, rows_spilt, mask_landed = (sems(n, 4) for n in
                                                                  ("gathered", "stored", "rows_back", "rows_spilt", "mask_landed"))

        def slice_of(ap, t, width):
            return ap[:, bass.ds(t.n * width, width)]

        consts_in, ident_made, consts_made = sem("consts_in"), sem("ident_made"), sem("consts_made")
        idx_made, place_made = sem("idx_made"), sem("place_made")
        keys_cleared, keys_in = sem("keys_cleared"), sem("keys_in")
        sorted_step, turned_sort, copied_sort = sem("sorted_step"), sem("turned_sort"), sem("copied_sort")
        keys_out, neighbours_in = sem("keys_out"), sem("neighbours_in")
        rows_max, starts_out, starts_in = sem("rows_max"), sem("starts_out"), sem("starts_in")
        before_made, before_out, before_in = sem("before_made"), sem("before_out"), sem("before_in")
        key_ready, mask_ready, pack_ready = sem("key_ready"), sem("mask_ready"), sem("pack_ready")
        mask_out, pack_out = sem("mask_out"), sem("pack_out")
        fields_ready, fields_turned, fields_taken = sem("fields_ready"), sem("fields_turned"), sem("fields_taken")
        pay_in = sem("pay_in")
        pay_cleared = sem("pay_cleared")
        quiet_col, quiet_done = sem("quiet_col"), sem("quiet_done")
        spare_out = sem("spare_out")
        index_chain = sem("index_chain")
        norm_rooted, coef_made, coef_rooted = sem("norm_rooted"), sem("coef_made"), sem("coef_rooted")
        sort_marks = []
        tables_ready = sem("tables_ready")

        block = ctx.enter_context(nc.Block())

        FULL = E // (2 * P)
        LEFT = E % (2 * P)

        def phases():
            layout = "q"
            for k in range(1, IDX_BITS + 1):
                yield ("flip", k)
                for b in range(k - 1, -1, -1):
                    want = "p" if b >= 7 else "q"
                    if want != layout:
                        yield ("turn", None)
                        layout = want
                    yield ("pair", b if b < 7 else b - 7)
            assert layout == "q"

        STEPS = list(phases())
        TURNS = sum(1 for kind, _ in STEPS if kind == "turn")

        d1_in, d1_out = sems("d1_in", 8), sems("d1_out", 4)

        def parts_of(t):
            return REST if t.last else P

        def dense1_sync(sp):
            def load(t):
                n = parts_of(t)
                if t.past(8):
                    sp.wait_ge(d1_ready.sem, d1_ready.base + t.n - 7)
                    sp.nop(nofuse=True)
                sp.dma_start(xin[0:n, t.slot(8), :], x_blocks[bass.ds(t.n * P, n), :]).then_inc(d1_in[t.slot(8)], 16)

            def store(t):
                n = parts_of(t)
                sp.wait_ge(d1_ready.sem, d1_ready.base + t.n + 1)
                sp.nop(nofuse=True)
                sp.dma_start(state_blocks[bass.ds(t.n * P, n), :],
                             rows_o[0:n, t.slot(4)].rearrange("p g d -> p (g d)")).then_inc(d1_out[t.slot(4)], 16)

            run_steps(sp, BLOCKS, [(0, load, 8), (6, store, 0)], 8)
            for s in range(4):
                sp.wait_ge(d1_out[s], 16 * len(range(s, BLOCKS, 4)))

        xin = sb("xin", [P, 8, ROW])

        def x_rows(t, ring=4):
            return xin[:, t.slot(ring), :].rearrange("p (g d) -> p g d", g=G)

        def dense1_vector(v):
            na = norm_a.begin("d1")

            def stats(t):
                v.wait_ge(d1_in[t.slot(8)], t.round(8) * 16 + 16)
                na.stats(v, t, x_rows(t, 8), parts_of(t))

            def scale(t):
                na.scale(v, t, parts_of(t))

            def add(t):
                n = parts_of(t)
                v.wait_ge(d1_mm.sem, d1_mm.base + t.n + 1)
                if t.past(4):
                    v.wait_ge(d1_out[t.slot(4)], t.round(4) * 16)
                v.tensor_tensor(rows_o[0:n, t.slot(4), :, 0:P],
                                banks[4 + t.slot(2)][0:n, :].rearrange("p (g d) -> p g d", g=G),
                                x_rows(t, 8)[0:n], ALU.add).then_inc(d1_ready.sem, 1)

            run_steps(v, BLOCKS, [(0, stats), (1, scale), (3, add)], 8)

        def dense1_scalar(a):
            na = norm_a.begin("d1")

            def copy(t):
                s, n = t.slot(2), parts_of(t)
                a.wait_ge(na.turned, na.base + t.n + 1)
                if t.past(2):
                    a.wait_ge(d1_mm.sem, d1_mm.base + t.n - 1)
                nc.scalar.activation(feat_a[:, s, :].rearrange("p (g d) -> p g d", g=G)[:, :, 0:n],
                                     banks[s][:, :].rearrange("p (g d) -> p g d", g=G)[:, :, 0:n],
                                     ACT.Copy).then_inc(d1_copied.sem, 1)

            run_steps(a, BLOCKS, [(0, lambda t: na.root(a, t, parts_of(t))),
                                  (1, lambda t: na.relu(a, t, x_rows(t, 8), parts_of(t))), (2, copy)], 8)

        def dense1_tensor(p):
            na = norm_a.begin("d1")

            def product(t):
                s, n = t.slot(2), parts_of(t)
                p.wait_ge(d1_copied.sem, d1_copied.base + t.n + 1)
                if t.past(2):
                    p.wait_ge(d1_ready.sem, d1_ready.base + t.n - 1)
                nc.tensor.matmul(banks[4 + s][0:n, :], ones_row[0:1, 0:n], bias_rows[0:1, 0, :], start=True, stop=False)
                for g in range(G):
                    last = nc.tensor.matmul(banks[4 + s][0:n, g * P:(g + 1) * P], feat_a[:, s, g * P:g * P + n],
                                            W["wself"][:, :], start=False, stop=(g == G - 1))
                last.then_inc(d1_mm.sem, 1)

            run_steps(p, BLOCKS, [(1, lambda t: na.turn(p, t, d1_copied, parts_of(t))), (2, product)], 8)

        l0_in, l0_out = Ring(gathered_a, 64, 0), Ring(stored, 64, 0)
        mask_in0, mask_in1, mask_in2, mask_in3 = (Ring(mask_landed, 16, i) for i in range(4))

        def mask_load(sp, which, scanned, landed):
            def load(t):
                if t.past(4):
                    sp.wait_ge(scanned.sem, scanned.base + t.n - 3)
                    sp.nop(nofuse=True)
                sp.dma_start(mask[:, t.slot(4), :],
                             mask_line[which:which + 1, bass.ds(t.n * ROW, ROW)].to_broadcast([P, ROW])
                             ).then_inc(landed[t.slot(4)], 16)
            return load

        def masks_sync(sp, which, scanned, landed):
            run_steps(sp, CHUNKS, [(0, mask_load(sp, which, scanned, landed))])

        def stage(pool, t, slot_ap, table, done):
            nc.gpsimd.tensor_copy(slot_ap, slice_of(table, t, G)).then_inc(done.sem, 1)

        def scan(v, t, op, mask_sems, bank, dest, scanned, read_by):
            s = t.slot(2)
            v.wait_ge(mask_sems[t.slot(4)], mask_sems.base(t.slot(4)) + t.round(4) * 16 + 16)
            if t.past(2):
                v.wait_ge(read_by.sem, read_by.base + t.n - 1)
            if t.past(1):
                v.wait_ge(scanned.sem, scanned.base + t.n)
                begin = dest[:, 1 - s, ROW - 1:ROW]
            else:
                begin = 0.0
            v.tensor_tensor_scan(dest[:, s, :], mask[:, t.slot(4), :], bank, begin, ALU.mult, op).then_inc(scanned.sem, 1)

        def layer0_pool(pool, nmax, nrows):
            def gather(t):
                s = t.slot(4)
                if t.past(4):
                    pool.wait_ge(l0_in[s], l0_in.base(s) + t.round(4) * 64)
                    pool.nop(nofuse=True)
                stage(pool, t, index[:, s, 0, :], dst_s_t, l0_staged)
                pool.wait_ge(l0_staged.sem, l0_staged.base + t.n + 1)
                pool.nop(nofuse=True)
                if t.past(4):
                    pool.wait_ge(norm_a.rows, norm_a.base + t.n - 3)
                    pool.nop(nofuse=True)
                for g in range(G):
                    pool.indirect_dma_start(out=rows_a[:, s, g, 0:P], out_offset=None, in_=x,
                                            in_offset=bass.IndirectOffsetOnAxis(ap=index[:, s, 0, g:g + 1], axis=0),
                                            bounds_check=nmax, oob_is_err=False).then_inc(l0_in[s], 16)

            def scatter(t):
                s = t.slot(4)
                if t.past(4):
                    pool.wait_ge(l0_out[s], l0_out.base(s) + t.round(4) * 64)
                    pool.nop(nofuse=True)
                stage(pool, t, index[:, s, 1, :], end_t[:, 0, :], l0_staged2)
                stage(pool, t, rows_o[:, s, :, P + 1], count_t[:, 0, :], l0_counts)
                pool.wait_ge(l0_staged2.sem, l0_staged2.base + t.n + 1)
                pool.wait_ge(l0_counts.sem, l0_counts.base + t.n + 1)
                pool.wait_ge(l0_ready.sem, l0_ready.base + t.n + 1)
                pool.nop(nofuse=True)
                for g in range(G):
                    pool.indirect_dma_start(out=state, out_offset=bass.IndirectOffsetOnAxis(ap=index[:, s, 1, g:g + 1], axis=0),
                                            in_=rows_o[:, s, g, :], in_offset=None, compute_op=ALU.add,
                                            bounds_check=nrows, oob_is_err=True).then_inc(l0_out[s], 16)

            norm_a.begin("l0")
            run_steps(pool, CHUNKS, [(0, gather), (5, scatter)])
            for s in range(4):
                pool.wait_ge(l0_out[s], l0_out.base(s) + 64 * len(range(s, CHUNKS, 4)))

        def layer0_vector(v):
            na = norm_a.begin("l0")

            def stats(t):
                v.wait_ge(l0_in[t.slot(4)], l0_in.base(t.slot(4)) + t.round(4) * 64 + 64)
                na.stats(v, t, rows_a[:, t.slot(4)])

            def maxima(t):
                v.wait_ge(na.turned, na.base + t.n + 1)
                scan(v, t, ALU.max, mask_in0, banks[t.slot(2)][:, :], feat_a, scanned0, l0_mm)

            run_steps(v, CHUNKS, [(0, stats), (1, lambda t: na.scale(v, t)), (2, maxima)])

        def layer0_scalar(a):
            na = norm_a.begin("l0")

            def copy(t):
                a.wait_ge(l0_mm.sem, l0_mm.base + t.n + 1)
                if t.past(4):
                    a.wait_ge(l0_out[t.slot(4)], l0_out.base(t.slot(4)) + t.round(4) * 64)
                nc.scalar.activation(rows_o[:, t.slot(4), :, 0:P],
                                     banks[4 + t.slot(2)][:, :].rearrange("p (g d) -> p g d", g=G),
                                     ACT.Copy).then_inc(l0_ready.sem, 1)

            run_steps(a, CHUNKS, [(0, lambda t: na.root(a, t)),
                                  (1, lambda t: na.relu(a, t, rows_a[:, t.slot(4)])), (3, copy)])

        def layer0_tensor(p):
            na = norm_a.begin("l0")

            def product(t):
                s = t.slot(2)
                p.wait_ge(scanned0.sem, scanned0.base + t.n + 1)
                if t.past(2):
                    p.wait_ge(l0_ready.sem, l0_ready.base + t.n - 1)
                for g in range(G):
                    last = nc.tensor.matmul(banks[4 + s][:, g * P:(g + 1) * P], feat_a[:, s, g * P:(g + 1) * P],
                                            W["wneigh"][:, :], start=True, stop=True)
                last.then_inc(l0_mm.sem, 1)

            run_steps(p, CHUNKS, [(1, lambda t: na.turn(p, t, scanned0)), (3, product)])

        d2_in, d2_out3, d2_out = sems("d2_in", 8), sems("d2_out3_", 4), sems("d2_out", 4)
        len_small = sb("len_small", [P, 2, 2, G])
        square = sb("square", [P, G, P])
        leaky = feat_b

        def dense2_sync(sp):
            def load(t):
                n = parts_of(t)
                if t.past(8):
                    sp.wait_ge(d2_x3.sem, d2_x3.base + t.n - 7)
                    sp.nop(nofuse=True)
                sp.dma_start(rows_ab[0:n, t.slot(8)].rearrange("p g d -> p (g d)"),
                             state_blocks[bass.ds(t.n * P, n), :]).then_inc(d2_in[t.slot(8)], 16)

            def store(t):
                n = parts_of(t)
                sp.wait_ge(d2_ready.sem, d2_ready.base + t.n + 1)
                sp.nop(nofuse=True)
                sp.dma_start(state3_blocks[bass.ds(t.n * P, n), :], xin[0:n, t.slot(4), :]).then_inc(d2_out3[t.slot(4)], 16)
                sp.dma_start(out_blocks[bass.ds(t.n * P, n), :], final[0:n, t.slot(4), :]).then_inc(d2_out[t.slot(4)], 16)

            run_steps(sp, BLOCKS, [(0, load, 8), (6, store, 0)], 8)
            for s in range(4):
                sp.wait_ge(d2_out3[s], 16 * len(range(s, BLOCKS, 4)))
                sp.wait_ge(d2_out[s], 16 * len(range(s, BLOCKS, 4)))

        final = feat_cd

        def dense2_vector(v):
            na = norm_a.begin("d2")

            def stats(t):
                v.wait_ge(d2_in[t.slot(8)], t.round(8) * 16 + 16)
                na.stats(v, t, rows_ab[:, t.slot(8)], parts_of(t))

            def leak(t):
                s, n = t.slot(2), parts_of(t)
                v.wait_ge(d2_fifth.sem, d2_fifth.base + t.n + 1)
                v.tensor_tensor(leaky[0:n, s, :], leaky[0:n, s, :], banks[4 + s][0:n, :], ALU.max).then_inc(d2_leaky.sem, 1)

            def finish(t):
                s, n = t.slot(2), parts_of(t)
                v.wait_ge(d2_root.sem, d2_root.base + t.n + 1)
                v.tensor_scalar(len_small[0:n, s, 1], len_small[0:n, s, 1], 1e-12, None, ALU.max).then_inc(d2_chain.sem, 1)
                v.wait_ge(d2_chain.sem, d2_chain.base + t.n + 1)
                v.reciprocal(len_small[0:n, s, 1], len_small[0:n, s, 1]).then_inc(d2_inv.sem, 1)
                v.wait_ge(d2_inv.sem, d2_inv.base + t.n + 1)
                if t.past(4):
                    v.wait_ge(d2_out3[t.slot(4)], t.round(4) * 16)
                    v.wait_ge(d2_out[t.slot(4)], t.round(4) * 16)
                for g in range(G):
                    last = v.scalar_tensor_tensor(xin[0:n, t.slot(4), g * P:(g + 1) * P], leaky[0:n, s, g * P:(g + 1) * P],
                                                  len_small[0:n, s, 1, g:g + 1], rows_ab[0:n, t.slot(8), g, 0:P],
                                                  ALU.mult, ALU.add)
                last.then_inc(d2_x3.sem, 1)
                v.wait_ge(d2_x3.sem, d2_x3.base + t.n + 1)
                v.tensor_tensor(final[0:n, t.slot(4), :], xin[0:n, t.slot(4), :], quiet[0:n, :], ALU.add).then_inc(d2_ready.sem, 1)

            run_steps(v, BLOCKS, [(0, stats), (1, lambda t: na.scale(v, t, parts_of(t))), (2, leak), (3, finish)], 8)

        def dense2_scalar(a):
            na = norm_a.begin("d2")

            def copy(t):
                s, n = t.slot(2), parts_of(t)
                a.wait_ge(na.turned, na.base + t.n + 1)
                if t.past(2):
                    a.wait_ge(d2_mm.sem, d2_mm.base + t.n - 1)
                nc.scalar.activation(feat_a[:, s, :].rearrange("p (g d) -> p g d", g=G)[:, :, 0:n],
                                     banks[s][:, :].rearrange("p (g d) -> p g d", g=G)[:, :, 0:n],
                                     ACT.Copy).then_inc(d2_copied.sem, 1)

            def lengths(t):
                s, n = t.slot(2), parts_of(t)
                a.wait_ge(d2_mm.sem, d2_mm.base + t.n + 1)
                if t.past(2):
                    a.wait_ge(d2_x3.sem, d2_x3.base + t.n - 1)
                nc.scalar.activation(leaky[0:n, s, :], banks[4 + s][0:n, :], ACT.Copy, scale=0.2).then_inc(d2_fifth.sem, 1)

            def squares(t):
                s, n = t.slot(2), parts_of(t)
                a.wait_ge(d2_leaky.sem, d2_leaky.base + t.n + 1)
                for g in range(G):
                    last = nc.scalar.activation(square[0:n, g, :], leaky[0:n, s, g * P:(g + 1) * P], ACT.Square,
                                                accum_out=len_small[0:n, s, 0, g:g + 1])
                last.then_inc(d2_norm.sem, 1)
                a.wait_ge(d2_norm.sem, d2_norm.base + t.n + 1)
                nc.scalar.activation(len_small[0:n, s, 1], len_small[0:n, s, 0], ACT.Sqrt).then_inc(d2_root.sem, 1)

            run_steps(a, BLOCKS, [(0, lambda t: na.root(a, t, parts_of(t))),
                                  (1, lambda t: na.relu(a, t, rows_ab[:, t.slot(8)], parts_of(t))), (2, copy), (2, lengths), (3, squares)], 8)

        def dense2_tensor(p):
            na = norm_a.begin("d2")

            def product(t):
                s, n = t.slot(2), parts_of(t)
                p.wait_ge(d2_copied.sem, d2_copied.base + t.n + 1)
                if t.past(2):
                    p.wait_ge(d2_leaky.sem, d2_leaky.base + t.n - 1)
                for g in range(G):
                    last = nc.tensor.matmul(banks[4 + s][0:n, g * P:(g + 1) * P], feat_a[:, s, g * P:g * P + n],
                                            W["m1w"][:, :], start=True, stop=True)
                last.then_inc(d2_mm.sem, 1)

            run_steps(p, BLOCKS, [(1, lambda t: na.turn(p, t, d2_copied, parts_of(t))), (2, product)], 8)

        l1_src_in, l1_dst_in, l1_spilt = Ring(gathered_a, 64, 1), sems("l1_dst_in", 4), Ring(rows_spilt, 16, 0)

        def layer1a_sync(sp):
            def spill(t):
                s = t.slot(4)
                sp.wait_ge(l1_dst_in[s], t.round(4) * 64 + 64)
                sp.nop(nofuse=True)
                sp.dma_start(dst_rows[bass.ds(t.n, 1)].rearrange("o p (g d) -> (o p) g d", g=G),
                             rows_b[:, s, :, 0:P]).then_inc(l1_spilt[s], 16)
            run_steps(sp, CHUNKS, [(0, spill)])
            for s in range(4):
                sp.wait_ge(l1_spilt[s], l1_spilt.base(s) + 16 * len(range(s, CHUNKS, 4)))

        def layer1a_pool(pool, nmax):
            def gather(t):
                s = t.slot(4)
                if t.past(4):
                    pool.wait_ge(l1_src_in[s], l1_src_in.base(s) + t.round(4) * 64)
                    pool.wait_ge(l1_dst_in[s], t.round(4) * 64)
                    pool.nop(nofuse=True)
                stage(pool, t, index[:, s, 0, :], src_t, l1_staged)
                stage(pool, t, index[:, s, 1, :], dst_t, l1_staged_d)
                pool.wait_ge(l1_staged.sem, l1_staged.base + t.n + 1)
                pool.wait_ge(l1_staged_d.sem, l1_staged_d.base + t.n + 1)
                if t.past(4):
                    pool.wait_ge(norm_a.rows, norm_a.base + t.n - 3)
                    pool.wait_ge(norm_b.rows, norm_b.base + t.n - 3)
                    pool.wait_ge(l1_degs.sem, l1_degs.base + t.n - 3)
                    pool.wait_ge(l1_spilt[s], l1_spilt.base(s) + t.round(4) * 16)
                pool.nop(nofuse=True)
                for rows, k, landed in ((rows_a, 0, l1_src_in), (rows_b, 1, l1_dst_in)):
                    for g in range(G):
                        pool.indirect_dma_start(out=rows[:, s, g, :], out_offset=None, in_=state[0:N, :],
                                                in_offset=bass.IndirectOffsetOnAxis(ap=index[:, s, k, g:g + 1], axis=0),
                                                bounds_check=nmax, oob_is_err=False).then_inc(landed[s], 16)
            norm_a.begin("l1")
            norm_b.begin("l1")
            run_steps(pool, CHUNKS, [(0, gather)])

        def bn_stats_of(v, t, ready):
            width = TAIL if t.last else ROW
            v.wait_ge(ready.sem, ready.base + t.n + 1)
            v.nop(nofuse=True)
            if t.last:
                v.bn_stats(bn_parts[:, t.n, :], hidden[:, t.n * ROW:t.n * ROW + width])
            else:
                v.bn_stats(bn_parts[:, bass.ds(t.n, 1), :].rearrange("p o s -> p (o s)"),
                           hidden[:, bass.ds(t.n * ROW, ROW)])

        def layer1a_vector(v):
            na, nb = norm_a.begin("l1"), norm_b.begin("l1")

            def stats(t):
                s = t.slot(4)
                v.wait_ge(l1_src_in[s], l1_src_in.base(s) + t.round(4) * 64 + 64)
                na.stats(v, t, rows_a[:, s])
                v.wait_ge(l1_dst_in[s], t.round(4) * 64 + 64)
                nb.stats(v, t, rows_b[:, s])
                v.tensor_copy(slice_of(deg_s_t, t, G), rows_a[:, s, :, P + 1])
                v.tensor_copy(slice_of(deg_d_t, t, G), rows_b[:, s, :, P + 1]).then_inc(l1_degs.sem, 1)

            def scale(t):
                na.scale(v, t)
                nb.scale(v, t)

            run_steps(v, CHUNKS, [(0, stats), (1, scale), (3, lambda t: bn_stats_of(v, t, l1_hidden))])

        def layer1a_scalar(a):
            na, nb = norm_a.begin("l1"), norm_b.begin("l1")

            def copy(t):
                s = t.slot(2)
                if t.past(2):
                    a.wait_ge(l1_mm.sem, l1_mm.base + t.n - 1)
                a.wait_ge(na.turned, na.base + t.n + 1)
                nc.scalar.activation(feat_a[:, s, :], banks[s][:, :], ACT.Copy)
                a.wait_ge(nb.turned, nb.base + t.n + 1)
                nc.scalar.activation(feat_b[:, s, :], banks[2 + s][:, :], ACT.Copy).then_inc(l1_copied.sem, 1)

            def keep(t):
                a.wait_ge(l1_mm.sem, l1_mm.base + t.n + 1)
                a.nop(nofuse=True)
                nc.scalar.activation(slice_of(hidden, t, ROW), banks[4 + t.slot(2)][:, :], ACT.Identity,
                                     bias=cols[:, E1B:E1B + 1]).then_inc(l1_hidden.sem, 1)

            def root(t):
                na.root(a, t)
                nb.root(a, t)

            def relu(t):
                na.relu(a, t, rows_a[:, t.slot(4)])
                nb.relu(a, t, rows_b[:, t.slot(4)])

            run_steps(a, CHUNKS, [(0, root), (1, relu), (2, copy), (3, keep)])

        def layer1a_tensor(p):
            na, nb = norm_a.begin("l1"), norm_b.begin("l1")

            def turn(t):
                na.turn(p, t, l1_copied)
                nb.turn(p, t, l1_copied)

            def product(t):
                s = t.slot(2)
                p.wait_ge(l1_copied.sem, l1_copied.base + t.n + 1)
                if t.past(2):
                    p.wait_ge(l1_hidden.sem, l1_hidden.base + t.n - 1)
                nc.tensor.matmul(banks[4 + s][:, :], W["e1s"][:, :], feat_a[:, s, :], start=True, stop=False)
                nc.tensor.matmul(banks[4 + s][:, :], W["e1d"][:, :], feat_b[:, s, :], start=False, stop=True).then_inc(l1_mm.sem, 1)

            run_steps(p, CHUNKS, [(1, turn), (2, product)])

        bn_sems = [[sem(f"bn{i}_{n}") for n in ("agg", "root", "chain")] for i in range(2)]
        bn_done = sems("bn_done", 2)

        def batch_norm_vector(v, which, gamma, beta):
            agg, root, chain = bn_sems[which]
            v.drain().then_inc(chain, 1)
            v.wait_ge(chain, 1)
            v.bn_aggr(bn_mv[:, :], bn_parts[:, :, :].rearrange("p c s -> p (c s)")).then_inc(agg, 1)
            v.wait_ge(root, 1)
            v.reciprocal(bn_sd[:, :], bn_sd[:, :]).then_inc(chain, 1)
            v.wait_ge(chain, 2)
            v.tensor_tensor(bn_scale[:, :], bn_sd[:, :], cols[:, gamma:gamma + 1], ALU.mult).then_inc(chain, 1)
            v.wait_ge(chain, 3)
            v.tensor_tensor(bn_tmp[:, :], bn_mv[:, 0:1], bn_scale[:, :], ALU.mult).then_inc(chain, 1)
            v.wait_ge(chain, 4)
            v.tensor_tensor(bn_shift[:, :], cols[:, beta:beta + 1], bn_tmp[:, :], ALU.subtract).then_inc(bn_done[which], 1)

        def batch_norm_scalar(a, which):
            agg, root, _ = bn_sems[which]
            a.wait_ge(agg, 1)
            nc.scalar.activation(bn_sd[:, :], bn_mv[:, 1:2], ACT.Sqrt, bias=eps_col[:, 0:1]).then_inc(root, 1)
            a.wait_ge(bn_done[which], 1)


        def layer1b_scalar(a):
            def act(t):
                if t.past(2):
                    a.wait_ge(l1b_mm.sem, l1b_mm.base + t.n - 1)
                a.nop(nofuse=True)
                nc.scalar.activation(feat_a[:, t.slot(2), :], slice_of(hidden, t, ROW), ACT.Relu,
                                     bias=bn_shift[:, 0:1], scale=bn_scale[:, 0:1]).then_inc(l1b_act.sem, 1)

            def keep(t):
                a.wait_ge(l1b_mm.sem, l1b_mm.base + t.n + 1)
                a.nop(nofuse=True)
                nc.scalar.activation(slice_of(hidden, t, ROW), banks[t.slot(2)][:, :], ACT.Identity,
                                     bias=cols[:, E2B:E2B + 1]).then_inc(l1b_hidden.sem, 1)

            run_steps(a, CHUNKS, [(0, act), (1, keep)])

        def layer1b_tensor(p):
            def product(t):
                s = t.slot(2)
                p.wait_ge(l1b_act.sem, l1b_act.base + t.n + 1)
                if t.past(2):
                    p.wait_ge(l1b_hidden.sem, l1b_hidden.base + t.n - 1)
                nc.tensor.matmul(banks[s][:, :], W["e2"][:, :], feat_a[:, s, :], start=True, stop=True).then_inc(l1b_mm.sem, 1)
            run_steps(p, CHUNKS, [(0, product)])

        def layer1b_vector(v):
            run_steps(v, CHUNKS, [(0, lambda t: bn_stats_of(v, t, l1b_hidden))])

        l1c_rows, l1c_spilt, l1c_out = Ring(rows_back, 16, 0), Ring(rows_spilt, 16, 1), Ring(stored, 64, 1)

        def row_load(sp, used, landed):
            def load(t):
                if t.past(4):
                    sp.wait_ge(used.sem, used.base + t.n - 3)
                    sp.nop(nofuse=True)
                sp.dma_start(xin[:, t.slot(4), :], dst_rows[bass.ds(t.n, 1)].rearrange("o p f -> (o p) f")
                             ).then_inc(landed[t.slot(4)], 16)
            return load

        def row_spill(sp, ready, spilt):
            def spill(t):
                sp.wait_ge(ready.sem, ready.base + t.n + 1)
                sp.nop(nofuse=True)
                sp.dma_start(dst_rows[bass.ds(t.n, 1)].rearrange("o p (g d) -> (o p) g d", g=G),
                             rows_o[:, t.slot(4), :, 0:P]).then_inc(spilt[t.slot(4)], 16)
            return spill

        def layer1c_sync(sp):
            run_steps(sp, CHUNKS, [(0, mask_load(sp, 1, scanned1, mask_in1)), (0, row_load(sp, l1c_ready, l1c_rows)),
                                   (3, row_spill(sp, l1c_ready, l1c_spilt))])
            for s in range(4):
                sp.wait_ge(l1c_spilt[s], l1c_spilt.base(s) + 16 * len(range(s, CHUNKS, 4)))

        def layer1c_scalar(a):
            def act(t):
                if t.past(2):
                    a.wait_ge(scanned1.sem, scanned1.base + t.n - 1)
                a.nop(nofuse=True)
                nc.scalar.activation(feat_a[:, t.slot(2), :], slice_of(hidden, t, ROW), ACT.Relu,
                                     bias=bn_shift[:, 0:1], scale=bn_scale[:, 0:1]).then_inc(l1c_act.sem, 1)
            run_steps(a, CHUNKS, [(0, act)])

        def layer1c_vector(v):
            def sums(t):
                v.wait_ge(l1c_act.sem, l1c_act.base + t.n + 1)
                scan(v, t, ALU.add, mask_in1, feat_a[:, t.slot(2), :], feat_b, scanned1, l1c_turned)

            def add(t):
                s = t.slot(4)
                v.wait_ge(l1c_turned.sem, l1c_turned.base + t.n + 1)
                v.wait_ge(l1c_rows[s], l1c_rows.base(s) + t.round(4) * 16 + 16)
                if t.past(4):
                    v.wait_ge(l1c_out[s], l1c_out.base(s) + t.round(4) * 64)
                    v.wait_ge(l1c_spilt[s], l1c_spilt.base(s) + t.round(4) * 16)
                v.tensor_tensor(rows_o[:, s, :, 0:P], banks[t.slot(2)][:, :].rearrange("p (g d) -> p g d", g=G),
                                x_rows(t), ALU.add).then_inc(l1c_ready.sem, 1)

            run_steps(v, CHUNKS, [(0, sums), (1, add)])

        def layer1c_tensor(p):
            def turn(t):
                s = t.slot(2)
                p.wait_ge(scanned1.sem, scanned1.base + t.n + 1)
                if t.past(2):
                    p.wait_ge(l1c_ready.sem, l1c_ready.base + t.n - 1)
                for g in range(G):
                    last = nc.tensor.transpose(banks[s][:, g * P:(g + 1) * P], feat_b[:, s, g * P:(g + 1) * P], ident[:, :])
                last.then_inc(l1c_turned.sem, 1)
            run_steps(p, CHUNKS, [(0, turn)])

        def layer1c_pool(pool, nmax):
            def scatter(t):
                s = t.slot(4)
                if t.past(4):
                    pool.wait_ge(l1c_out[s], l1c_out.base(s) + t.round(4) * 64)
                    pool.nop(nofuse=True)
                stage(pool, t, index[:, s, 1, :], end_t[:, 1, :], l1c_staged)
                stage(pool, t, rows_o[:, s, :, P], count_t[:, 1, :], l1c_facts)
                stage(pool, t, rows_o[:, s, :, P + 1], deg_d_t, l1c_facts2)
                pool.wait_ge(l1c_staged.sem, l1c_staged.base + t.n + 1)
                pool.wait_ge(l1c_facts.sem, l1c_facts.base + t.n + 1)
                pool.wait_ge(l1c_facts2.sem, l1c_facts2.base + t.n + 1)
                pool.wait_ge(l1c_ready.sem, l1c_ready.base + t.n + 1)
                pool.nop(nofuse=True)
                for g in range(G):
                    pool.indirect_dma_start(out=state[0:N, :],
                                            out_offset=bass.IndirectOffsetOnAxis(ap=index[:, s, 1, g:g + 1], axis=0),
                                            in_=rows_o[:, s, g, :], in_offset=None,
                                            bounds_check=nmax, oob_is_err=False).then_inc(l1c_out[s], 16)
            run_steps(pool, CHUNKS, [(0, scatter)])
            for s in range(4):
                pool.wait_ge(l1c_out[s], l1c_out.base(s) + 64 * len(range(s, CHUNKS, 4)))

        l2_in, l2_rows, l2_spilt, l2_out = Ring(gathered_a, 64, 2), Ring(rows_back, 16, 1), Ring(rows_spilt, 16, 2), Ring(stored, 64, 2)

        def layer2_sync(sp):
            run_steps(sp, CHUNKS, [(0, mask_load(sp, 1, scanned2, mask_in2)), (0, row_load(sp, l2_ready, l2_rows)),
                                   (4, row_spill(sp, l2_ready, l2_spilt))])
            for s in range(4):
                sp.wait_ge(l2_spilt[s], l2_spilt.base(s) + 16 * len(range(s, CHUNKS, 4)))

        def edge_pool(pool, nmax, source, width, gathered, staged, fact, facts_done, facts_used,
                      target, out_sems, ready, staged2, lag):
            def gather(t):
                s = t.slot(4)
                if t.past(4):
                    pool.wait_ge(gathered[s], gathered.base(s) + t.round(4) * 64)
                    pool.wait_ge(facts_used.sem, facts_used.base + t.n - 3)
                    pool.nop(nofuse=True)
                stage(pool, t, index[:, s, 0, :], src_t, staged)
                stage(pool, t, facts[:, s, 0, :], fact, facts_done)
                pool.wait_ge(staged.sem, staged.base + t.n + 1)
                if t.past(4):
                    pool.wait_ge(norm_a.rows, norm_a.base + t.n - 3)
                pool.nop(nofuse=True)
                for g in range(G):
                    pool.indirect_dma_start(out=rows_a[:, s, g, 0:width], out_offset=None, in_=source,
                                            in_offset=bass.IndirectOffsetOnAxis(ap=index[:, s, 0, g:g + 1], axis=0),
                                            bounds_check=nmax, oob_is_err=False).then_inc(gathered[s], 16)

            def scatter(t):
                s = t.slot(4)
                if t.past(4):
                    pool.wait_ge(out_sems[s], out_sems.base(s) + t.round(4) * 64)
                    pool.nop(nofuse=True)
                stage(pool, t, index[:, s, 1, :], end_t[:, 1, :], staged2)
                pool.wait_ge(staged2.sem, staged2.base + t.n + 1)
                pool.wait_ge(ready.sem, ready.base + t.n + 1)
                pool.nop(nofuse=True)
                for g in range(G):
                    pool.indirect_dma_start(out=target, out_offset=bass.IndirectOffsetOnAxis(ap=index[:, s, 1, g:g + 1], axis=0),
                                            in_=rows_o[:, s, g, 0:P], in_offset=None,
                                            bounds_check=nmax, oob_is_err=False).then_inc(out_sems[s], 16)
            run_steps(pool, CHUNKS, [(0, gather), (lag, scatter)])
            for s in range(4):
                pool.wait_ge(out_sems[s], out_sems.base(s) + 64 * len(range(s, CHUNKS, 4)))

        def layer2_pool(pool, nmax):
            norm_a.begin("l2")
            edge_pool(pool, nmax, state[0:N, :], XW, l2_in, l2_staged, norm_t, l2_facts, l2_scaled,
                      state3, l2_out, l2_ready, l2_staged2, 5)

        def layer2_vector(v):
            na, nb = norm_a.begin("l2"), norm_b.begin("l2")

            def stats(t):
                s = t.slot(4)
                v.wait_ge(l2_in[s], l2_in.base(s) + t.round(4) * 64 + 64)
                na.stats(v, t, rows_a[:, s], degree=rows_a[:, s, :, P])
                v.wait_ge(l2_rows[s], l2_rows.base(s) + t.round(4) * 16 + 16)
                nb.stats(v, t, x_rows(t))

            def scale(t):
                na.scale(v, t)
                nb.scale(v, t)

            def sums(t):
                s = t.slot(2)
                v.wait_ge(na.turned, na.base + t.n + 1)
                scan(v, t, ALU.add, mask_in2, banks[s][:, :], feat_a, scanned2, l2_mm)
                v.wait_ge(scanned2.sem, scanned2.base + t.n + 1)
                v.wait_ge(l2_copied.sem, l2_copied.base + t.n + 1)
                v.tensor_tensor(feat_c[:, s, :], feat_a[:, s, :], feat_b[:, s, :], ALU.mult).then_inc(l2_prod.sem, 1)

            def total(t):
                s = t.slot(2)
                v.wait_ge(l2_scaled.sem, l2_scaled.base + t.n + 1)
                v.tensor_tensor(feat_d[:, s, :], banks[6 + s][:, :], feat_d[:, s, :], ALU.add).then_inc(l2_sum.sem, 1)
                v.wait_ge(l2_sum.sem, l2_sum.base + t.n + 1)
                v.scalar_tensor_tensor(feat_d[:, s, :], feat_d[:, s, :], 0.2, feat_d[:, s, :],
                                       ALU.mult, ALU.max).then_inc(l2_leaky.sem, 1)

            def finish(t):
                s, r = t.slot(2), t.slot(4)
                v.wait_ge(l2_root.sem, l2_root.base + t.n + 1)
                v.tensor_scalar(len_small[:, s, 1], len_small[:, s, 1], 1e-12, None, ALU.max).then_inc(l2_chain.sem, 1)
                v.wait_ge(l2_chain.sem, l2_chain.base + t.n * 2 + 1)
                v.reciprocal(len_small[:, s, 1], len_small[:, s, 1]).then_inc(l2_chain.sem, 1)
                v.wait_ge(l2_chain.sem, l2_chain.base + t.n * 2 + 2)
                if t.past(4):
                    v.wait_ge(l2_out[r], l2_out.base(r) + t.round(4) * 64)
                    v.wait_ge(l2_spilt[r], l2_spilt.base(r) + t.round(4) * 16)
                for g in range(G):
                    last = v.scalar_tensor_tensor(rows_o[:, r, g, 0:P], feat_d[:, s, g * P:(g + 1) * P],
                                                  len_small[:, s, 1, g:g + 1], x_rows(t)[:, g, :], ALU.mult, ALU.add)
                last.then_inc(l2_ready.sem, 1)

            run_steps(v, CHUNKS, [(0, stats), (1, scale), (3, finish), (2, sums), (2, total)])

        def layer2_scalar(a):
            na, nb = norm_a.begin("l2"), norm_b.begin("l2")

            def root(t):
                na.root(a, t, degree=True)
                nb.root(a, t)

            def relu(t):
                na.relu(a, t, rows_a[:, t.slot(4)])
                nb.relu(a, t, x_rows(t))

            def copy(t):
                s = t.slot(2)
                if t.past(2):
                    a.wait_ge(l2_mm.sem, l2_mm.base + t.n - 1)
                a.wait_ge(nb.turned, nb.base + t.n + 1)
                nc.scalar.activation(feat_b[:, s, :], banks[2 + s][:, :], ACT.Copy).then_inc(l2_copied.sem, 1)

            def message(t):
                s = t.slot(2)
                a.wait_ge(l2_mm.sem, l2_mm.base + t.n + 1)
                a.wait_ge(l2_facts.sem, l2_facts.base + t.n + 1)
                if t.past(2):
                    a.wait_ge(l2_ready.sem, l2_ready.base + t.n - 1)
                for g in range(G):
                    last = nc.scalar.activation(feat_d[:, s, g * P:(g + 1) * P], banks[4 + s][:, g * P:(g + 1) * P],
                                                ACT.Copy, scale=facts[:, t.slot(4), 0, g:g + 1])
                last.then_inc(l2_scaled.sem, 1)

            def lengths(t):
                s = t.slot(2)
                a.wait_ge(l2_leaky.sem, l2_leaky.base + t.n + 1)
                for g in range(G):
                    last = nc.scalar.activation(square[:, g, :], feat_d[:, s, g * P:(g + 1) * P], ACT.Square,
                                                accum_out=len_small[:, s, 0, g:g + 1])
                last.then_inc(l2_norm.sem, 1)
                a.wait_ge(l2_norm.sem, l2_norm.base + t.n + 1)
                nc.scalar.activation(len_small[:, s, 1], len_small[:, s, 0], ACT.Sqrt).then_inc(l2_root.sem, 1)

            run_steps(a, CHUNKS, [(0, root), (1, relu), (2, copy), (2, message), (2, lengths)])

        def layer2_tensor(p):
            na, nb = norm_a.begin("l2"), norm_b.begin("l2")

            def turn(t):
                na.turn(p, t, scanned2)
                nb.turn(p, t, l2_copied)

            def product(t):
                s = t.slot(2)
                p.wait_ge(l2_prod.sem, l2_prod.base + t.n + 1)
                if t.past(2):
                    p.wait_ge(l2_sum.sem, l2_sum.base + t.n - 1)
                for g in range(G):
                    cut = slice(g * P, (g + 1) * P)
                    nc.tensor.matmul(banks[4 + s][:, cut], feat_a[:, s, cut], W["m1w"][:, :], start=True, stop=False)
                    nc.tensor.matmul(banks[4 + s][:, cut], feat_c[:, s, cut], W["m2w"][:, :], start=False, stop=True)
                    last = nc.tensor.matmul(banks[6 + s][:, cut], feat_b[:, s, cut], W["m1w"][:, :], start=True, stop=True)
                last.then_inc(l2_mm.sem, 1)

            run_steps(p, CHUNKS, [(1, turn), (2, product)])

        l3_in, l3_rows, l3_out = Ring(gathered_a, 64, 3), Ring(rows_back, 16, 2), Ring(stored, 64, 3)

        def layer3_sync(sp):
            run_steps(sp, CHUNKS, [(0, mask_load(sp, 1, scanned3, mask_in3)), (0, row_load(sp, l3_ready, l3_rows))])

        def layer3_pool(pool, nmax):
            norm_a.begin("l3")
            edge_pool(pool, nmax, state3, P, l3_in, l3_staged, coef_t, l3_facts, l3_coef,
                      out, l3_out, l3_ready, l3_staged2, 6)

        def layer3_vector(v):
            na = norm_a.begin("l3")

            def stats(t):
                s = t.slot(4)
                v.wait_ge(l3_in[s], l3_in.base(s) + t.round(4) * 64 + 64)
                na.stats(v, t, rows_a[:, s])

            def weigh(t):
                s = t.slot(2)
                v.wait_ge(na.rows, na.base + t.n + 1)
                v.wait_ge(l3_facts.sem, l3_facts.base + t.n + 1)
                for g in range(G):
                    last = v.tensor_scalar(na.tile[:, s, g, :], na.tile[:, s, g, :], facts[:, t.slot(4), 0, g:g + 1], None, ALU.mult)
                last.then_inc(l3_coef.sem, 1)

            def sums(t):
                v.wait_ge(na.turned, na.base + t.n + 1)
                scan(v, t, ALU.add, mask_in3, banks[t.slot(2)][:, :], feat_a, scanned3, l3_mm1)

            def add(t):
                s = t.slot(4)
                v.wait_ge(l3_mm2.sem, l3_mm2.base + t.n + 1)
                v.wait_ge(l3_rows[s], l3_rows.base(s) + t.round(4) * 16 + 16)
                if t.past(4):
                    v.wait_ge(l3_out[s], l3_out.base(s) + t.round(4) * 64)
                v.tensor_tensor(rows_o[:, s, :, 0:P], banks[4 + t.slot(2)][:, :].rearrange("p (g d) -> p g d", g=G),
                                x_rows(t), ALU.add).then_inc(l3_ready.sem, 1)

            run_steps(v, CHUNKS, [(0, stats), (1, lambda t: na.scale(v, t)), (2, weigh), (3, sums), (4, add)])

        def layer3_scalar(a):
            na = norm_a.begin("l3")

            def act(t):
                s = t.slot(2)
                a.wait_ge(l3_mm1.sem, l3_mm1.base + t.n + 1)
                if t.past(2):
                    a.wait_ge(l3_mm2.sem, l3_mm2.base + t.n - 1)
                nc.scalar.activation(feat_b[:, s, :], banks[2 + s][:, :], ACT.Relu, bias=cols[:, C1B:C1B + 1]).then_inc(l3_act.sem, 1)

            run_steps(a, CHUNKS, [(0, lambda t: na.root(a, t)), (1, lambda t: na.relu(a, t, rows_a[:, t.slot(4)])), (3, act)])

        def layer3_tensor(p):
            na = norm_a.begin("l3")

            def first(t):
                s = t.slot(2)
                p.wait_ge(scanned3.sem, scanned3.base + t.n + 1)
                if t.past(2):
                    p.wait_ge(l3_act.sem, l3_act.base + t.n - 1)
                nc.tensor.matmul(banks[2 + s][:, :], W["c1w"][:, :], feat_a[:, s, :], start=True, stop=True).then_inc(l3_mm1.sem, 1)

            def second(t):
                s = t.slot(2)
                p.wait_ge(l3_act.sem, l3_act.base + t.n + 1)
                if t.past(2):
                    p.wait_ge(l3_ready.sem, l3_ready.base + t.n - 1)
                nc.tensor.matmul(banks[4 + s][:, :], ones_row[0:1, :], bias_rows[0:1, 1, :], start=True, stop=False)
                for g in range(G):
                    last = nc.tensor.matmul(banks[4 + s][:, g * P:(g + 1) * P], feat_b[:, s, g * P:(g + 1) * P],
                                            W["c2w"][:, :], start=False, stop=(g == G - 1))
                last.then_inc(l3_mm2.sem, 1)

            run_steps(p, CHUNKS, [(2, lambda t: na.turn(p, t, scanned3, ready=l3_coef)), (3, first), (4, second)])

        def payload_pool(pool, emax):
            pool.wait_ge(pay_cleared, 1)
            for i in range(2):
                def gather(t, i=i):
                    s = t.slot(4)
                    if t.past(4):
                        pool.wait_ge(pay_slots[i][s], t.round(4) * 64)
                        pool.nop(nofuse=True)
                    stage(pool, t, index[:, s, i, :], idx_t[:, i, :], pay_staged[i])
                    pool.wait_ge(pay_staged[i].sem, t.n + 1)
                    if t.past(4):
                        pool.wait_ge(pay_taken[i], t.n - 3)
                    pool.nop(nofuse=True)
                    for g in range(G):
                        pool.indirect_dma_start(out=pay_in_rows[:, i, s, g, :], out_offset=None, in_=payload,
                                                in_offset=bass.IndirectOffsetOnAxis(ap=index[:, s, i, g:g + 1], axis=0),
                                                bounds_check=emax, oob_is_err=False).then_inc(pay_slots[i][s], 16)

                def take(t, i=i):
                    s = t.slot(4)
                    pool.wait_ge(pay_slots[i][s], t.round(4) * 64 + 64)
                    pool.nop(nofuse=True)
                    nc.gpsimd.tensor_copy(pay[:, i, bass.ds(t.n * G, G), :], pay_in_rows[:, i, s, :, :]).then_inc(pay_taken[i], 1)

                run_steps(pool, CHUNKS, [(0, gather), (3, take)])
            pool.wait_ge(pay_taken[0], CHUNKS)
            pool.wait_ge(pay_taken[1], CHUNKS)
            nc.gpsimd.tensor_copy(dst_s_t[:, :], pay[:, 0, :, 1])
            nc.gpsimd.tensor_copy(src_t[:, :], pay[:, 1, :, 0])
            nc.gpsimd.tensor_copy(dst_t[:, :], pay[:, 1, :, 1]).then_inc(tables_ready, 1)

        pay_in_rows = sb("pay_in_rows", [P, 2, 4, G, 4])
        pay_slots = [sems(f"pay_slot{i}_", 4) for i in range(2)]
        pay_staged, pay_taken = [Count(m, 0) for m in sems("pay_staged", 2)], sems("pay_taken", 2)

        @block.sync
        def _(sp):
            for n, a in (("wself", wself_t), ("wneigh", wneigh_t), ("e1s", e1_src_t), ("e1d", e1_dst_t),
                         ("e2", e2_t), ("m1w", m1), ("m2w", m2), ("c1w", c1), ("c2w", c2)):
                sp.dma_start(W[n][:, :], a).then_inc(consts_in, 16)
            for i, a in enumerate((e1_b, e1_g, e1_be, e2_b, e2_g, e2_be, c1_b)):
                sp.dma_start(cols[:, i:i + 1], a.rearrange("(p o) -> p o", o=1)).then_inc(consts_in, 16)
            for i, a in enumerate((bias0, c2_b)):
                for g in range(G):
                    sp.dma_start(bias_rows[0:1, i, g * P:(g + 1) * P],
                                 a.rearrange("(o p) -> o p", o=1)).then_inc(consts_in, 16)
            sp.wait_ge(keys_cleared, 1)
            for i, a in enumerate((src, dst)):
                sp.dma_start(keys[0:FULL, i, :], a[0:FULL * 2 * P].rearrange("(r f) -> r f", f=2 * P)).then_inc(keys_in, 16)
                if LEFT:
                    sp.dma_start(keys[FULL:FULL + 1, i, 0:LEFT],
                                 a[FULL * 2 * P:E].rearrange("(r f) -> r f", r=1)).then_inc(keys_in, 16)
            sp.dma_start(weights_in[0:FULL, :],
                         edge_weight[0:FULL * 2 * P].rearrange("(r f) -> r f", f=2 * P)).then_inc(keys_in, 16)
            if LEFT:
                sp.dma_start(weights_in[FULL:FULL + 1, 0:LEFT],
                             edge_weight[FULL * 2 * P:E].rearrange("(r f) -> r f", r=1)).then_inc(keys_in, 16)
            sp.wait_ge(consts_made, 1)
            spare = state[N:N + TILES * P, :].rearrange("(c p g) d -> c p (g d)", p=P, g=G)
            with sp.Fori(0, CHUNKS) as c:
                sp.dma_start(spare[bass.ds(c, 1)].rearrange("o p f -> (o p) f"), zero_rows[:, :]).then_inc(spare_out, 16)
            for i in range(2):
                sp.dma_start(key_line[i:i + 1, 0:1], minus1[0:1, :]).then_inc(keys_out, 16)
                sp.dma_start(key_line[i:i + 1, SORT + 1:SORT + 2], minus1[0:1, :]).then_inc(keys_out, 16)
                sp.dma_start(start_line[i:i + 1, 0:1], zero2[0:1, :]).then_inc(starts_out, 16)
            sp.wait_ge(pack_ready, 1)
            sp.dma_start(payload[0:FULL * 2 * P, :].rearrange("(r f) w -> r (f w)", f=2 * P),
                         pack[0:FULL, :, :].rearrange("p f w -> p (f w)")).then_inc(pack_out, 16)
            if LEFT:
                sp.dma_start(payload[FULL * 2 * P:E, :].rearrange("(r f) w -> r (f w)", r=1),
                             pack[FULL:FULL + 1, 0:LEFT, :].rearrange("p f w -> p (f w)")).then_inc(pack_out, 16)
            line_view = "(h q p) -> q h p"
            sp.wait_ge(key_ready, 1)
            for i in range(2):
                sp.dma_start(key_line[i, 1:SORT + 1].rearrange(line_view, h=2, q=P),
                             key_f[:, i, :].rearrange("q (h p) -> q h p", h=2)).then_inc(keys_out, 16)
            sp.wait_ge(keys_out, 16 * 6)
            for i in range(2):
                sp.dma_start(prev_f[:, i, :].rearrange("q (h p) -> q h p", h=2),
                             key_line[i, 0:SORT].rearrange(line_view, h=2, q=P)).then_inc(neighbours_in, 16)
                sp.dma_start(next_f[:, i, :].rearrange("q (h p) -> q h p", h=2),
                             key_line[i, 2:SORT + 2].rearrange(line_view, h=2, q=P)).then_inc(neighbours_in, 16)
            sp.wait_ge(mask_ready, 1)
            for i in range(2):
                sp.dma_start(mask_line[i, :].rearrange(line_view, h=2, q=P),
                             mask_b[:, i, :].rearrange("q (h p) -> q h p", h=2)).then_inc(mask_out, 16)
            sp.wait_ge(rows_max, 1)
            with nc.allow_non_contiguous_dma(reason="256 single values"):
                for i in range(2):
                    for h in range(2):
                        sp.dma_start(start_line[i, 1 + h * P:1 + (h + 1) * P].rearrange("(q o) -> q o", o=1),
                                     row_max[:, i, h:h + 1]).then_inc(starts_out, 16)
                sp.wait_ge(starts_out, 16 * 6)
                sp.dma_start(line[:, :], start_line[:, 0:2 * P]).then_inc(starts_in, 16)
                sp.wait_ge(before_made, 1)
                sp.dma_start(before_line, line2[:, :]).then_inc(before_out, 16)
                sp.wait_ge(before_out, 16)
                for i in range(2):
                    for h in range(2):
                        sp.dma_start(row_before[:, i, h:h + 1],
                                     before_line[i, h * P:(h + 1) * P].rearrange("(q o) -> q o", o=1)).then_inc(before_in, 16)
            sp.wait_ge(mask_out, 32)
            sp.wait_ge(pack_out, 32 if LEFT else 16)
            sp.wait_ge(spare_out, 16 * CHUNKS)
            phase_end(sp, "index")

            dense1_sync(sp)
            phase_end(sp, "dense1")
            masks_sync(sp, 0, scanned0, mask_in0)
            phase_end(sp, "layer0")
            dense2_sync(sp)
            phase_end(sp, "dense2")
            layer1a_sync(sp)
            phase_end(sp, "layer1a")
            phase_end(sp, "layer1b")
            layer1c_sync(sp)
            phase_end(sp, "layer1c")
            layer2_sync(sp)
            phase_end(sp, "layer2")
            layer3_sync(sp)
            phase_end(sp, "layer3")

        @block.gpsimd
        def _(pool):
            g = nc.gpsimd
            g.memset(ident[:, :], 0.0).then_inc(ident_made, 1)
            pool.wait_ge(ident_made, 1)
            g.affine_select(out=ident[:, :], in_=ident[:, :], compare_op=ALU.not_equal, fill=1.0, base=0,
                            pattern=[[-1, P]], channel_multiplier=1).then_inc(ident_made, 1)
            g.iota(place[:, :], pattern=[[1, 2 * P]], base=0, channel_multiplier=2 * P).then_inc(idx_made, 1)
            g.iota(gray[:, :].rearrange("q (h p) -> q h p", h=2), pattern=[[P * P, 2], [1, P]], base=0,
                   channel_multiplier=P).then_inc(place_made, 1)
            phase_end(pool, "index")
            nmax, emax, rmax = pool.to_reg(N - 1), pool.to_reg(E - 1), pool.to_reg(N + TILES * P - 1)
            payload_pool(pool, emax)
            phase_end(pool, "dense1")
            layer0_pool(pool, nmax, rmax)
            phase_end(pool, "layer0")
            phase_end(pool, "dense2")
            layer1a_pool(pool, nmax)
            phase_end(pool, "layer1a")
            phase_end(pool, "layer1b")
            layer1c_pool(pool, nmax)
            phase_end(pool, "layer1c")
            layer2_pool(pool, nmax)
            phase_end(pool, "layer2")
            layer3_pool(pool, nmax)
            phase_end(pool, "layer3")

        @block.vector
        def _(v):
            done = [0]

            def link(ins):
                done[0] += 1
                ins.then_inc(sorted_step, 1)
                v.wait_ge(sorted_step, done[0])

            v.memset(keys[:, :, :], PAD_KEY)
            v.memset(weights_in[:, :], 0.0).then_inc(keys_cleared, 1)
            v.memset(zero_rows[:, :], 0.0)
            v.memset(ones_row[:, :], 1.0)
            v.memset(minus1[:, :], -1.0)
            v.memset(zero2[:, :], 0.0)
            v.memset(eps_col[:, :], LN_EPS)
            v.memset(rows_ab[:, :, :, :], 0.0)
            v.memset(rows_o[:, :, :, :], 0.0)
            v.memset(pay_in_rows[:, :, :, :, :], 0.0)
            v.memset(pack[:, :, :], 0.0).then_inc(pay_cleared, 1)
            v.drain().then_inc(consts_made, 1)

            v.wait_ge(keys_in, 16 * (6 if LEFT else 3))
            v.wait_ge(consts_made, 1)
            v.tensor_copy(pack[:, :, 0], keys[:, 0, :])
            v.tensor_copy(pack[:, :, 1], keys[:, 1, :])
            v.tensor_copy(pack[:, :, 2], weights_in[:, :]).then_inc(pack_ready, 1)
            link(v.tensor_scalar(tmp_f[:, :, :], keys[:, :, :], float(HALF), float(LIFT), ALU.is_ge, ALU.mult))
            link(v.scalar_tensor_tensor(tmp_i[:, :, :], keys[:, :, :], 256.0, tmp_f[:, :, :], ALU.add, ALU.add))
            link(v.tensor_scalar(tmp_i[:, :, :], tmp_i[:, :, :], IDX_BITS, None, ALU.logical_shift_left))
            v.wait_ge(idx_made, 1)
            for i in range(2):
                ins = v.tensor_tensor(sort_a[:, i, :].bitcast(I32), tmp_i[:, i, :], place[:, :], ALU.bitwise_or)
            link(ins)
            v.wait_ge(place_made, 1)
            link(v.tensor_copy(place_f[:, :], gray[:, :]))
            link(v.tensor_scalar(place[:, :], gray[:, :], 1, None, ALU.logical_shift_left))
            here, there = sort_a, sort_b
            turns = 0
            for kind, k in STEPS:
                if kind == "flip":
                    if k == 1:
                        link(v.tensor_scalar(flip[:, :], gray[:, :], 30, -2 ** 31, ALU.logical_shift_left, ALU.bitwise_and))
                        link(v.tensor_tensor(gray[:, :], gray[:, :], place[:, :], ALU.bitwise_xor))
                    else:
                        link(v.tensor_scalar(flip[:, :], gray[:, :], 31 - k, -2 ** 31, ALU.logical_shift_left, ALU.bitwise_and))
                    for i in range(2):
                        ins = v.tensor_tensor(here[:, i, :].bitcast(I32), here[:, i, :].bitcast(I32), flip[:, :], ALU.bitwise_xor)
                    link(ins)
                elif kind == "turn":
                    turns += 1
                    v.wait_ge(copied_sort, turns)
                    here, there = there, here
                elif kind == "pair":
                    a = here[:, :, :].rearrange("q s (o two i) -> q (s o) two i", two=2, i=1 << k)
                    b = there[:, :, :].rearrange("q s (o two i) -> q (s o) two i", two=2, i=1 << k)
                    v.tensor_tensor(b[:, :, 0, :], a[:, :, 0, :], a[:, :, 1, :], ALU.max)
                    link(v.tensor_tensor(b[:, :, 1, :], a[:, :, 0, :], a[:, :, 1, :], ALU.min))
                    here, there = there, here
                sort_marks.append((kind, done[0], here is sort_a))
            result = here

            link(v.tensor_scalar(tmp_i[:, :, :], result[:, :, :].bitcast(I32), (1 << IDX_BITS) - 1, None, ALU.bitwise_and))
            link(v.tensor_copy(idx_f[:, :, :], tmp_i[:, :, :]))
            link(v.tensor_scalar(tmp_i[:, :, :], result[:, :, :].bitcast(I32), IDX_BITS, (1 << 17) - 1,
                                 ALU.logical_shift_right, ALU.bitwise_and))
            link(v.tensor_scalar(tmp_f[:, :, :], tmp_i[:, :, :], 65536.0, float(-LIFT), ALU.is_ge, ALU.mult))
            v.scalar_tensor_tensor(key_f[:, :, :], tmp_i[:, :, :], -256.0, tmp_f[:, :, :], ALU.add, ALU.add).then_inc(key_ready, 1)
            v.wait_ge(key_ready, 1)
            v.wait_ge(neighbours_in, 64)
            v.tensor_tensor(mask_b[:, :, :], key_f[:, :, :], prev_f[:, :, :], ALU.is_equal).then_inc(mask_ready, 1)
            link(v.tensor_tensor(first_f[:, :, :], key_f[:, :, :], prev_f[:, :, :], ALU.not_equal))
            for i in range(2):
                ins = v.tensor_tensor(first_f[:, i, :], first_f[:, i, :], place_f[:, :], ALU.mult)
            link(ins)
            for i in range(2):
                for h in range(2):
                    cut = slice(h * P, (h + 1) * P)
                    ins = v.tensor_tensor_scan(count_f[:, i, cut], first_f[:, i, cut], first_f[:, i, cut], 0.0, ALU.max, ALU.max)
            link(ins)
            v.tensor_copy(row_max[:, :, :], count_f[:, :, :].rearrange("q s (h p) -> q s h p", h=2)[:, :, :, P - 1]).then_inc(rows_max, 1)
            link(v.tensor_tensor(end_f[:, :, :], key_f[:, :, :], next_f[:, :, :], ALU.not_equal))
            link(v.tensor_scalar(tmp_f[:, :, :], key_f[:, :, :], float(N), None, ALU.is_lt))
            link(v.tensor_tensor(end_f[:, :, :], end_f[:, :, :], tmp_f[:, :, :], ALU.mult))
            link(v.tensor_scalar(prev_f[:, 0, :], place_f[:, :], float(N), None, ALU.add))
            v.memset(prev_f[:, 1, :], float(FAR))
            link(v.drain())
            link(v.tensor_tensor(next_f[:, :, :], key_f[:, :, :], prev_f[:, :, :], ALU.subtract))
            link(v.tensor_tensor(next_f[:, :, :], next_f[:, :, :], end_f[:, :, :], ALU.mult))
            link(v.tensor_tensor(end_f[:, :, :], next_f[:, :, :], prev_f[:, :, :], ALU.add))
            v.wait_ge(starts_in, 16)
            v.tensor_tensor_scan(line2[:, :], line[:, :], line[:, :], 0.0, ALU.max, ALU.max).then_inc(before_made, 1)
            v.wait_ge(before_in, 64)
            for i in range(2):
                for h in range(2):
                    cut = slice(h * P, (h + 1) * P)
                    ins = v.tensor_scalar(first_f[:, i, cut], count_f[:, i, cut], row_before[:, i, h:h + 1], -1.0, ALU.max, ALU.mult)
            link(ins)
            for i in range(2):
                ins = v.scalar_tensor_tensor(count_f[:, i, :], first_f[:, i, :], 1.0, place_f[:, :], ALU.add, ALU.add)
            ins.then_inc(fields_ready, 1)

            for i, (field, table) in enumerate(((idx_f, idx_t), (end_f, end_t), (count_f, count_t))):
                v.wait_ge(fields_turned, i + 1)
                v.tensor_copy(table[:, :, :].rearrange("p s t -> p (s t)"), banks[i][:, :]).then_inc(fields_taken, 1)
            v.wait_ge(consts_in, 16 * 24)
            v.wait_ge(consts_made, 1)
            v.tensor_scalar(relu_b[:, :], zero_rows[:, 0:P], cols[:, C1B:C1B + 1], 0.0, ALU.add, ALU.max).then_inc(quiet_col, 1)
            v.wait_ge(quiet_done, 1)
            v.tensor_copy(quiet[:, :], banks[7][:, :])
            phase_end(v, "index")

            dense1_vector(v)
            phase_end(v, "dense1")
            layer0_vector(v)
            v.wait_ge(norm_rooted, 1)
            v.reciprocal(norm_t[:, :], norm_t[:, :])
            phase_end(v, "layer0")
            dense2_vector(v)
            phase_end(v, "dense2")
            layer1a_vector(v)
            batch_norm_vector(v, 0, E1G, E1BE)
            v.tensor_scalar(deg_s_t[:, :], deg_s_t[:, :], 1.0, None, ALU.max).then_inc(index_chain, 1)
            v.wait_ge(index_chain, 1)
            v.scalar_tensor_tensor(coef_t[:, :], deg_d_t[:, :], 1.0, deg_s_t[:, :], ALU.max, ALU.mult).then_inc(coef_made, 1)
            phase_end(v, "layer1a")
            layer1b_vector(v)
            batch_norm_vector(v, 1, E2G, E2BE)
            v.wait_ge(coef_rooted, 1)
            v.reciprocal(coef_t[:, :], coef_t[:, :]).then_inc(index_chain, 1)
            v.wait_ge(index_chain, 2)
            v.tensor_tensor(coef_t[:, :], coef_t[:, :], pay[:, 1, :, 2], ALU.mult)
            phase_end(v, "layer1b")
            layer1c_vector(v)
            phase_end(v, "layer1c")
            layer2_vector(v)
            phase_end(v, "layer2")
            layer3_vector(v)
            phase_end(v, "layer3")

        @block.scalar
        def _(a):
            turns = 0
            for kind, _, in_a in sort_marks:
                if kind == "turn":
                    turns += 1
                    a.wait_ge(turned_sort, turns)
                    target = sort_a if in_a else sort_b
                    nc.scalar.activation(target[:, :, :].rearrange("p s t -> p (s t)"), banks[turns % 2][:, :],
                                         ACT.Copy).then_inc(copied_sort, 1)
            phase_end(a, "index")
            dense1_scalar(a)
            phase_end(a, "dense1")
            nc.scalar.activation(norm_t[:, :], count_t[:, 1, 0:TILES], ACT.Sqrt).then_inc(norm_rooted, 1)
            layer0_scalar(a)
            phase_end(a, "layer0")
            dense2_scalar(a)
            phase_end(a, "dense2")
            layer1a_scalar(a)
            batch_norm_scalar(a, 0)
            a.wait_ge(coef_made, 1)
            nc.scalar.activation(coef_t[:, :], coef_t[:, :], ACT.Sqrt).then_inc(coef_rooted, 1)
            phase_end(a, "layer1a")
            layer1b_scalar(a)
            batch_norm_scalar(a, 1)
            phase_end(a, "layer1b")
            layer1c_scalar(a)
            phase_end(a, "layer1c")
            layer2_scalar(a)
            phase_end(a, "layer2")
            layer3_scalar(a)
            phase_end(a, "layer3")

        @block.tensor
        def _(p):
            p.wait_ge(ident_made, 2)
            turns = 0
            for kind, steps, in_a in sort_marks:
                if kind == "turn":
                    turns += 1
                    p.wait_ge(sorted_step, steps)
                    if turns > 2:
                        p.wait_ge(copied_sort, turns - 2)
                    origin = sort_b if in_a else sort_a
                    for j in range(4):
                        last = nc.tensor.transpose(banks[turns % 2][:, j * P:(j + 1) * P],
                                                   origin[:, j // 2, (j % 2) * P:(j % 2 + 1) * P], ident[:, :])
                    last.then_inc(turned_sort, 1)
            p.wait_ge(fields_ready, 1)
            for i, field in enumerate((idx_f, end_f, count_f)):
                for j in range(4):
                    last = nc.tensor.transpose(banks[i][:, j * P:(j + 1) * P],
                                               field[:, j // 2, (j % 2) * P:(j % 2 + 1) * P], ident[:, :])
                last.then_inc(fields_turned, 1)
            p.wait_ge(quiet_col, 1)
            nc.tensor.matmul(banks[7][:, :], ones_row[0:1, :], bias_rows[0:1, 1, :], start=True, stop=False)
            for j in range(G):
                last = nc.tensor.matmul(banks[7][:, j * P:(j + 1) * P], relu_b[:, :], W["c2w"][:, :], start=False, stop=(j == G - 1))
            last.then_inc(quiet_done, 1)
            phase_end(p, "index")
            dense1_tensor(p)
            phase_end(p, "dense1")
            layer0_tensor(p)
            phase_end(p, "layer0")
            dense2_tensor(p)
            phase_end(p, "dense2")
            layer1a_tensor(p)
            phase_end(p, "layer1a")
            layer1b_tensor(p)
            phase_end(p, "layer1b")
            layer1c_tensor(p)
            phase_end(p, "layer1c")
            layer2_tensor(p)
            phase_end(p, "layer2")
            layer3_tensor(p)
            phase_end(p, "layer3")


def kernel(**inputs):
    import numpy as _np
    import concourse.bacc as _bacc
    from concourse import mybir as _mybir
    from concourse.bass_utils import run_bass_kernel_spmd as _run

    i = {k: _np.asarray(v) for k, v in inputs.items()}
    D = i["x"].shape[1]
    laid = {
        "x": i["x"], "src": i["src"], "dst": i["dst"], "edge_weight": i["edge_weight"],
        "wself_t": i["L0_gnn_W"][:, :D].T, "wneigh_t": i["L0_gnn_W"][:, D:].T, "bias0": i["L0_gnn_b"],
        "e1_src_t": i["L1_gnn_W1"][:, :D].T, "e1_dst_t": i["L1_gnn_W1"][:, D:].T, "e1_b": i["L1_gnn_b1"],
        "e1_g": i["L1_gnn_g1"], "e1_be": i["L1_gnn_be1"],
        "e2_t": i["L1_gnn_W2"].T, "e2_b": i["L1_gnn_b2"], "e2_g": i["L1_gnn_g2"], "e2_be": i["L1_gnn_be2"],
        "m1": i["L2_gnn_W1"], "m2": i["L2_gnn_W2"],
        "c1": i["L3_gnn_W1"], "c1_b": i["L3_gnn_b1"], "c2": i["L3_gnn_W2"], "c2_b": i["L3_gnn_b2"],
    }
    nc = _bacc.Bacc("TRN2", target_bir_lowering=False, num_devices=1)
    arrays, args = {}, []
    for name, a in laid.items():
        a = _np.ascontiguousarray(a)
        arrays[f"in_{name}"] = a
        args.append(nc.dram_tensor(f"in_{name}", a.shape, _mybir.dt.from_np(a.dtype), kind="ExternalInput").ap())
    args.append(nc.dram_tensor("out_x", i["x"].shape, _mybir.dt.float32, kind="ExternalOutput").ap())
    build_gnn(nc, *args)
    r = _run(nc, [arrays], core_ids=[0])
    return r.results[0]["out_x"]
```

```python
from contextlib import ExitStack

import concourse.bass as bass
from concourse import mybir

F32 = mybir.dt.float32
I32 = mybir.dt.int32
BF16 = mybir.dt.bfloat16
ALU = mybir.AluOpType
ACT = mybir.ActivationFunctionType

P = 128
G = 4
ROW = G * P
XW = P + 2
LN_EPS = 1e-05
BN_EPS = 1e-05
SORT = 2 * P * P
IDX_BITS = 15
FAR = 1 << 20


class Turn:

    def __init__(self, group, off, last, unroll):
        self.group, self.off, self.last, self.unroll = group, off, last, unroll
        self.fixed = isinstance(group, int)
        self.n = group * unroll + off

    def slot(self, ring):
        return self.off % ring

    def round(self, ring):
        return self.group * (self.unroll // ring) + self.off // ring

    def past(self, steps):
        return not self.fixed or self.n >= steps


def run_steps(eng, count, stages, unroll=4, slow_count=0, slow=()):
    reach = max([lag + (more[0] if more else 4) for lag, _, *more in stages] + [4 * (lag + 2) for _, lag, _ in slow])
    stages = [(lag, stage) for lag, stage, *_ in stages]
    steps = max([count + lag for lag, _ in stages] + [4 * (slow_count + lag) for _, lag, _ in slow])
    first = -(-reach // unroll)
    last = (count - 1) // unroll
    if slow:
        last = min(last, 4 * (slow_count - 1) // unroll)
    last = max(last, first)

    def peeled(n):
        for lag, stage in stages:
            if 0 <= n - lag < count:
                stage(Turn(0, n - lag, n - lag == count - 1, unroll))
        for at, lag, stage in slow:
            if n % 4 == at and 0 <= n // 4 - lag < slow_count:
                stage(Turn(0, n // 4 - lag, n // 4 - lag == slow_count - 1, unroll // 4))

    for n in range(first * unroll if last > first else 0):
        peeled(n)
    if last > first:
        with eng.Fori(first, last) as group:
            for u in range(unroll):
                for lag, stage in stages:
                    stage(Turn(group, u - lag, False, unroll))
                for at, lag, stage in slow:
                    if u % 4 == at:
                        stage(Turn(group, u // 4 - lag, False, unroll // 4))
    for n in range(last * unroll if last > first else 0, steps):
        peeled(n)


def build_gnn(nc, x, src, dst, edge_weight, wself_t, wneigh_t, bias0, e1_src_t, e1_dst_t, e1_b, e1_g, e1_be,
              e2_t, e2_b, e2_g, e2_be, m1, m2, c1, c1_b, c2, c2_b, out):
    N = x.shape[0]
    E = src.shape[0]
    CHUNKS = -(-E // ROW)
    TILES = G * CHUNKS
    TAIL = E - (CHUNKS - 1) * ROW
    BLOCKS = -(-N // ROW)
    REST = (N - (BLOCKS - 1) * ROW) // G
    HALF = N // 2
    LIFT = (1 << 16) - HALF
    PAD_KEY = (1 << 16) + 60000 - 256 - LIFT
    assert (N - (BLOCKS - 1) * ROW) % G == 0 and HALF + 256 < 60000 and PAD_KEY >= N and E <= 1 << IDX_BITS

    def dram(name, shape, dt=F32):
        return nc.dram_tensor(name, shape, dt, kind="Internal").ap()

    state = dram("state", (N + TILES * P, XW))
    state3 = dram("state3", (N, P))
    dst_rows = dram("dst_rows", (CHUNKS, P, G * P))
    key_line = dram("key_line", (2, SORT + 2))
    mask_line = dram("mask_line", (2, SORT), BF16)
    start_line = dram("start_line", (2, 2 * P + 1))
    before_line = dram("before_line", (2, 2 * P))
    payload = dram("payload", (E, 4))

    x_blocks = x.rearrange("(a g) d -> a (g d)", g=G)
    state_blocks = state.rearrange("(a g) d -> a (g d)", g=G)
    state3_blocks = state3.rearrange("(a g) d -> a (g d)", g=G)
    out_blocks = out.rearrange("(a g) d -> a (g d)", g=G)

    with ExitStack() as ctx:
        def sb(name, shape, dt=F32):
            return ctx.enter_context(nc.sbuf_tensor(name, shape, dt))

        def sem(name):
            return ctx.enter_context(nc.semaphore(name))

        def sems(name, n):
            return [sem(f"{name}{i}") for i in range(n)]

        banks = [ctx.enter_context(nc.psum_tensor(f"bank{i}", [P, ROW], F32)) for i in range(8)]

        W = {n: sb(n, [P, P]) for n in ("wself", "wneigh", "e1s", "e1d", "e2", "m1w", "m2w", "c1w", "c2w")}
        cols = sb("cols", [P, 8])
        E1B, E1G, E1BE, E2B, E2G, E2BE, C1B = range(7)
        bias_parts = sb("bias_parts", [3, 2, ROW], BF16)
        ones3 = sb("ones3", [3, P], BF16)
        ident = sb("ident", [P, P])
        ones_row = sb("ones_row", [1, P])
        eps_col = sb("eps_col", [P, 1])
        quiet = sb("quiet", [P, ROW])

        hidden = sb("hidden", [P, max(CHUNKS * ROW, 26 * ROW + 2 * TILES * 4 + G * XW + P)])
        views = [0]

        def early(dt=F32, halves=2):
            at = views[0]
            views[0] += halves * 2 * P
            view = hidden[:, at:at + halves * 2 * P]
            view = view.bitcast(dt) if dt != F32 else view
            return view.rearrange("p (s f) -> p s f", s=2) if halves == 2 else view

        keys = early(I32)
        weights_in = early(halves=1)
        sort_a = early()
        sort_b = early()
        place = early(I32, 1)
        place_f = early(halves=1)
        gray = early(I32, 1)
        flip = early(I32, 1)
        tmp_i = early(I32)
        tmp_f = early()
        key_f = early()
        idx_f = early()
        prev_f = early()
        next_f = early()
        end_f = early()
        count_f = early()
        first_f = early()
        pack = early(halves=4).rearrange("p (f w) -> p f w", w=4)
        mask_b = sb("mask_b", [P, 2, 2 * P], BF16)
        row_max = sb("row_max", [P, 2, 2])
        row_before = sb("row_before", [P, 2, 2])
        line = sb("line", [2, 2 * P])
        line2 = sb("line2", [2, 2 * P])
        minus1 = sb("minus1", [2, 1])
        zero2 = sb("zero2", [2, 1])
        idx_t = early(I32)
        end_t = sb("end_t", [P, 2, 2 * P], I32)
        count_t = sb("count_t", [P, 2, 2 * P])
        pay = hidden[:, 19 * ROW:19 * ROW + 2 * TILES * 4].rearrange("p (s t w) -> p s t w", s=2, w=4)
        zero_rows = hidden[:, 19 * ROW + 2 * TILES * 4:][:, 0:G * XW]
        relu_b = hidden[:, 19 * ROW + 2 * TILES * 4 + G * XW:][:, 0:P]
        late = 19 * ROW + 2 * TILES * 4 + G * XW + P
        bias_rows = hidden[0:1, late:late + 2 * ROW].rearrange("p (i f) -> p i f", i=2)
        bias_left = hidden[0:1, late + 2 * ROW:late + 4 * ROW].rearrange("p (i f) -> p i f", i=2)
        bias_split = hidden[0:1, late + 4 * ROW:late + 7 * ROW].bitcast(BF16).rearrange("p (k i f) -> p k i f", k=3, i=2)
        weight_t = sb("weight_t", [P, TILES])
        dst_s_t = sb("dst_s_t", [P, TILES], I32)
        src_t = sb("src_t", [P, TILES], I32)
        dst_t = sb("dst_t", [P, TILES], I32)
        norm_t = sb("norm_t", [P, TILES])
        coef_t = sb("coef_t", [P, TILES])
        deg_s_t = sb("deg_s_t", [P, TILES])
        deg_d_t = sb("deg_d_t", [P, TILES])

        rows_ab = sb("rows_ab", [P, 8, G, XW])
        rows_a, rows_b = rows_ab[:, 0:4], rows_ab[:, 4:8]
        rows_o = sb("rows_o", [P, 4, G, XW])
        mask = sb("mask", [P, 4, ROW], BF16)
        index = sb("index", [P, 4, 2, G], I32)
        facts = sb("facts", [P, 4, 2, G])
        feat_a = sb("feat_a", [P, 2, ROW])
        feat_b4 = sb("feat_b4", [P, 4, ROW])
        feat_b = feat_b4[:, 0:2]
        feat_cd = sb("feat_cd", [P, 4, ROW])
        feat_ends = sb("feat_ends", [P, 2, ROW])
        bn_parts = sb("bn_parts", [P, CHUNKS, 6])
        bn_mv = sb("bn_mv", [P, 2])
        bn_sd = sb("bn_sd", [P, 1])
        bn_scale = sb("bn_scale", [P, 1])
        bn_tmp = sb("bn_tmp", [P, 1])
        bn_shift = sb("bn_shift", [P, 1])

        PHASES = ["index", "dense1", "layer0", "layer1a", "layer1b", "layer1c", "layer2", "layer3"]
        engines_done = sem("engines_done")

        def phase_end(eng, name):
            at = PHASES.index(name) + 1
            eng.drain().then_inc(engines_done, 1)
            eng.wait_ge(engines_done, 5 * at)
            eng.nop(nofuse=True)

        class RowNorm:

            def __init__(self, name, banks_, phases, tile=None, fields=4):
                self.ring, self.fields = len(banks_), fields
                self.tile = sb(name + "_h", [P, self.ring, G, P]) if tile is None else tile
                self.stat = sb(name + "_stat", [P, fields, G, 6])
                self.small = sb(name + "_small", [P, fields, 8, G])
                self.banks = banks_
                self.phases = phases
                self.chain, self.var, self.rooted, self.inverted, self.scaled, self.rows, self.turned = (
                    sem(f"{name}_{k}") for k in ("chain", "var", "root", "inverse", "scaled", "rows", "turned"))

            def share(self, name, banks_, phases, slot=None):
                return RowNorm(name, banks_, phases, self.tile if slot is None else self.tile[:, slot:slot + 1], 2)

            def begin(self, phase):
                self.base = self.chain_base = 0
                for name, steps, self.links in self.phases:
                    if name == phase:
                        return self
                    self.base += steps
                    self.chain_base += steps * self.links
                raise KeyError(phase)

            def field(self, t, i, parts=P):
                return self.small[0:parts, t.slot(self.fields), i]

            def moments(self, v, t, rows, parts=P):
                for g in range(G):
                    last = v.bn_stats(self.stat[0:parts, t.slot(self.fields), g, :], rows[0:parts, g, 0:P])
                last.then_inc(self.chain, 1)

            def spread(self, v, t, parts=P):
                st = self.stat[0:parts, t.slot(self.fields)]
                v.wait_ge(self.chain, self.chain_base + t.n * self.links + 1)
                v.tensor_tensor(self.field(t, 0, parts), st[:, :, 1], st[:, :, 4], ALU.add)
                v.tensor_tensor(self.field(t, 1, parts), st[:, :, 1], st[:, :, 4], ALU.subtract)
                v.tensor_tensor(self.field(t, 2, parts), st[:, :, 2], st[:, :, 5], ALU.add).then_inc(self.chain, 1)

            def between(self, v, t, parts=P):
                diff = self.field(t, 1, parts)
                v.wait_ge(self.chain, self.chain_base + t.n * self.links + 2)
                v.scalar_tensor_tensor(self.field(t, 3, parts), diff, P / 4.0, diff, ALU.mult, ALU.mult).then_inc(self.chain, 1)

            def variance(self, v, t, parts=P, degree=None):
                q, d2, var = (self.field(t, i, parts) for i in (2, 3, 4))
                v.wait_ge(self.chain, self.chain_base + t.n * self.links + 3)
                if degree is None:
                    v.tensor_tensor(var, q, d2, ALU.add).then_inc(self.var, 1)
                    return
                v.tensor_tensor(d2, q, d2, ALU.add).then_inc(self.chain, 1)
                v.wait_ge(self.chain, self.chain_base + t.n * self.links + 4)
                v.tensor_scalar(d2, d2, 1.0 / P, LN_EPS, ALU.mult, ALU.add).then_inc(self.chain, 1)
                v.wait_ge(self.chain, self.chain_base + t.n * self.links + 5)
                v.scalar_tensor_tensor(var, degree, 1.0, d2, ALU.max, ALU.mult).then_inc(self.var, 1)

            def root(self, a, t, parts=P, degree=False):
                a.wait_ge(self.var, self.base + t.n + 1)
                if degree:
                    nc.scalar.activation(self.field(t, 7, parts), self.field(t, 4, parts), ACT.Sqrt).then_inc(self.rooted, 1)
                else:
                    nc.scalar.activation(self.field(t, 7, parts), self.field(t, 4, parts), ACT.Sqrt,
                                         bias=eps_col[0:parts, 0:1], scale=1.0 / P).then_inc(self.rooted, 1)

            def inverse(self, v, t, parts=P):
                v.wait_ge(self.rooted, self.base + t.n + 1)
                v.reciprocal(self.field(t, 5, parts), self.field(t, 7, parts)).then_inc(self.inverted, 1)

            def shift(self, v, t, parts=P):
                v.wait_ge(self.inverted, self.base + t.n + 1)
                v.scalar_tensor_tensor(self.field(t, 6, parts), self.field(t, 0, parts), -0.5, self.field(t, 5, parts),
                                       ALU.mult, ALU.mult).then_inc(self.scaled, 1)

            def affine(self, v, t, rows, done, parts=P, first=G):
                s = t.slot(self.ring)
                v.wait_ge(self.scaled, self.base + t.n + 1)
                if t.past(self.ring):
                    v.wait_ge(self.turned, self.base + t.n + 1 - self.ring)
                for g in range(first, G):
                    last = v.tensor_scalar(self.tile[0:parts, s, g, :], rows[0:parts, g, 0:P],
                                           self.field(t, 5, parts)[:, g:g + 1], self.field(t, 6, parts)[:, g:g + 1],
                                           ALU.mult, ALU.add)
                last.then_inc(done.sem, 1)

            def relu(self, a, t, rows, parts=P, until=G):
                s = t.slot(self.ring)
                a.wait_ge(self.scaled, self.base + t.n + 1)
                if t.past(self.ring):
                    a.wait_ge(self.turned, self.base + t.n + 1 - self.ring)
                for g in range(until):
                    last = nc.scalar.activation(self.tile[0:parts, s, g, :], rows[0:parts, g, 0:P], ACT.Relu,
                                                bias=self.field(t, 6, parts)[:, g:g + 1],
                                                scale=self.field(t, 5, parts)[:, g:g + 1])
                last.then_inc(self.rows, 1)

            def turn(self, p, t, taken, parts=P, ready=None, split=None):
                s = t.slot(self.ring)
                if split is not None:
                    p.wait_ge(split.sem, split.base + t.n + 1)
                if ready is None:
                    p.wait_ge(self.rows, self.base + t.n + 1)
                else:
                    p.wait_ge(ready.sem, ready.base + t.n + 1)
                if t.past(self.ring):
                    p.wait_ge(taken.sem, taken.base + t.n + 1 - self.ring)
                for g in range(G):
                    last = nc.tensor.transpose(self.banks[s][:, g * P:g * P + parts],
                                               self.tile[0:parts, s, g, :], ident[0:parts, 0:parts])
                last.then_inc(self.turned, 1)

        norm_a = RowNorm("na", banks[0:2], [("d1", BLOCKS, 3), ("l0", CHUNKS, 3), ("d2", BLOCKS, 3), ("l2", CHUNKS, 5), ("l3", CHUNKS, 3)])
        norm_b = RowNorm("nb", banks[2:4], [("l2", CHUNKS, 3)])
        norm_src = norm_b.share("ns", banks[5:6], [("l1", CHUNKS, 3)], 0)
        norm_dst = norm_b.share("nt", banks[6:7], [("l1", CHUNKS, 3)], 1)

        class Count:

            def __init__(self, semaphore, base):
                self.sem, self.base = semaphore, base

        def in_turn(name, *steps):
            shared, base, views = sem(name), 0, []
            for n in steps:
                views.append(Count(shared, base))
                base += n
            return views

        (d1_copied, l0_mm, d2_copied, l1b_act, l1c_act, l2_copied, l3_mm1) = in_turn("d1_copied_and_later", BLOCKS, CHUNKS, BLOCKS, CHUNKS, CHUNKS, CHUNKS, CHUNKS)
        (d1_mm, l0_ready, d2_mm, l1b_mm, l1c_turned, l2_mm, l3_mm2) = in_turn("d1_mm_and_later", BLOCKS, CHUNKS, BLOCKS, CHUNKS, CHUNKS, CHUNKS, CHUNKS)
        (d1_ready, l0_staged, d2_leaky, l1b_hidden, l1c_ready, l2_ready, l3_ready) = in_turn("d1_ready_and_later", BLOCKS, CHUNKS, BLOCKS, CHUNKS, CHUNKS, CHUNKS, CHUNKS)
        (l0_staged2, d2_norm, l1c_staged, l2_staged, l3_staged) = in_turn("l0_staged2_and_later", CHUNKS, BLOCKS, CHUNKS, CHUNKS, CHUNKS)
        (l0_counts, d2_root, l1c_facts, l2_staged2, l3_staged2) = in_turn("l0_counts_and_later", CHUNKS, BLOCKS, CHUNKS, CHUNKS, CHUNKS)
        (d2_inv, l1c_facts2, l2_facts, l3_facts) = in_turn("d2_inv_and_later", BLOCKS, CHUNKS, CHUNKS, CHUNKS)
        (scanned0, d2_x3, scanned1, scanned2, scanned3) = in_turn("scanned0_and_later", CHUNKS, BLOCKS, CHUNKS, CHUNKS, CHUNKS)
        (d2_ready, l2_prod, l3_coef) = in_turn("d2_ready_and_later", BLOCKS, CHUNKS, CHUNKS)
        (d2_chain, l2_chain, l3_act) = in_turn("d2_chain_and_later", BLOCKS, CHUNKS, CHUNKS)
        (d2_fifth, l2_scaled) = in_turn("d2_fifth_and_later", BLOCKS, CHUNKS)
        (l2_inv,) = in_turn("l2_inv_and_later", CHUNKS)
        (l2_sum,) = in_turn("l2_sum_and_later", CHUNKS)
        (l2_leaky,) = in_turn("l2_leaky_and_later", CHUNKS)
        (l2_norm,) = in_turn("l2_norm_and_later", CHUNKS)
        (l2_root,) = in_turn("l2_root_and_later", CHUNKS)

        d2_share = Count(sem("d2_share"), 0)
        D2_SHARE = 2
        l1_copied, l1_copied_d, l1_mm, l1_hidden, l1_degs, l1_staged, l1_staged_d = (
            Count(sem(n), 0) for n in ("l1_copied", "l1_copied_d", "l1_mm", "l1_hidden", "l1_degs", "l1_staged", "l1_staged_d"))

        class Ring:

            def __init__(self, slots, per_step, phase):
                self.slots, self.per_step, self.phase = slots, per_step, phase

            def __getitem__(self, slot):
                return self.slots[slot]

            def base(self, slot):
                return self.phase * self.per_step * len(range(slot, CHUNKS, 4))

        gathered_a, stored, rows_back, rows_spilt, mask_landed = (sems(n, 4) for n in
                                                                  ("gathered", "stored", "rows_back", "rows_spilt", "mask_landed"))

        def slice_of(ap, t, width):
            return ap[:, bass.ds(t.n * width, width)]

        consts_in, ident_made, consts_made = sem("consts_in"), sem("ident_made"), sem("consts_made")
        idx_made, place_made = sem("idx_made"), sem("place_made")
        keys_cleared, keys_in = sem("keys_cleared"), sem("keys_in")
        sorted_step, turned_sort, copied_sort = sem("sorted_step"), sem("turned_sort"), sem("copied_sort")
        keys_out, neighbours_in = sem("keys_out"), sem("neighbours_in")
        rows_max, starts_out, starts_in = sem("rows_max"), sem("starts_out"), sem("starts_in")
        before_made, before_out, before_in = sem("before_made"), sem("before_out"), sem("before_in")
        key_ready, mask_ready, pack_ready = sem("key_ready"), sem("mask_ready"), sem("pack_ready")
        mask_out, pack_out = sem("mask_out"), sem("pack_out")
        fields_ready, fields_turned, fields_taken = sem("fields_ready"), sem("fields_turned"), sem("fields_taken")
        pay_cleared = sem("pay_cleared")
        quiet_col, quiet_done = sem("quiet_col"), sem("quiet_done")
        spare_out = sem("spare_out")
        bias_ready, bias_in = sem("bias_ready"), sem("bias_in")
        index_chain = sem("index_chain")
        norm_rooted, coef_made, coef_rooted = sem("norm_rooted"), sem("coef_made"), sem("coef_rooted")
        sort_marks = []
        tables_ready = sem("tables_ready")

        block = ctx.enter_context(nc.Block())

        FULL = E // (2 * P)
        LEFT = E % (2 * P)

        def phases():
            layout = "q"
            for k in range(1, IDX_BITS + 1):
                yield ("flip", k)
                for b in range(k - 1, -1, -1):
                    want = "p" if b >= 7 else "q"
                    if want != layout:
                        yield ("turn", None)
                        layout = want
                    yield ("pair", b if b < 7 else b - 7)
            assert layout == "q"

        STEPS = list(phases())
        TURNS = sum(1 for kind, _ in STEPS if kind == "turn")

        dense_in, dense_out = sems("dense_in", 8), sems("dense_out", 4)

        def d2_base(per_step, slot, ring):
            return per_step * len(range(slot, BLOCKS, ring))

        def parts_of(t):
            return REST if t.last else P

        def dense1_sync(sp):
            def load(t):
                n = parts_of(t)
                if t.past(8):
                    sp.wait_ge(d1_ready.sem, d1_ready.base + t.n - 7)
                    sp.nop(nofuse=True)
                sp.dma_start(xin[0:n, t.slot(8), :], x_blocks[bass.ds(t.n * P, n), :]).then_inc(dense_in[t.slot(8)], 16)

            def store(t):
                n = parts_of(t)
                sp.wait_ge(d1_ready.sem, d1_ready.base + t.n + 1)
                sp.nop(nofuse=True)
                sp.dma_start(state_blocks[bass.ds(t.n * P, n), :],
                             rows_o[0:n, t.slot(4)].rearrange("p g d -> p (g d)")).then_inc(dense_out[t.slot(4)], 16)

            run_steps(sp, BLOCKS, [(0, load, 8), (7, store, 0)], 8)
            for s in range(4):
                sp.wait_ge(dense_out[s], 16 * len(range(s, BLOCKS, 4)))

        xin = sb("xin", [P, 8, ROW])

        def x_rows(t, ring=4):
            return xin[:, t.slot(ring), :].rearrange("p (g d) -> p g d", g=G)

        def dense1_vector(v):
            na = norm_a.begin("d1")

            def stats(t):
                v.wait_ge(dense_in[t.slot(8)], t.round(8) * 16 + 16)
                na.moments(v, t, x_rows(t, 8), parts_of(t))

            def add(t):
                n = parts_of(t)
                v.wait_ge(d1_mm.sem, d1_mm.base + t.n + 1)
                if t.past(4):
                    v.wait_ge(dense_out[t.slot(4)], t.round(4) * 16)
                v.tensor_tensor(rows_o[0:n, t.slot(4), :, 0:P],
                                banks[4 + t.slot(4)][0:n, :].rearrange("p (g d) -> p g d", g=G),
                                x_rows(t, 8)[0:n], ALU.add).then_inc(d1_ready.sem, 1)

            parts = parts_of
            run_steps(v, BLOCKS, [(0, stats), (2, lambda t: na.inverse(v, t, parts(t))), (0, lambda t: na.spread(v, t, parts(t))),
                                  (2, lambda t: na.shift(v, t, parts(t))), (0, lambda t: na.between(v, t, parts(t))),
                                  (5, add), (0, lambda t: na.variance(v, t, parts(t)))], 8)

        def dense1_scalar(a):
            na = norm_a.begin("d1")

            def copy(t):
                s, n = t.slot(2), parts_of(t)
                a.wait_ge(na.turned, na.base + t.n + 1)
                if t.past(2):
                    a.wait_ge(d1_mm.sem, d1_mm.base + t.n - 1)
                nc.scalar.activation(feat_a[:, s, :].rearrange("p (g d) -> p g d", g=G)[:, :, 0:n],
                                     banks[s][:, :].rearrange("p (g d) -> p g d", g=G)[:, :, 0:n],
                                     ACT.Copy).then_inc(d1_copied.sem, 1)

            run_steps(a, BLOCKS, [(1, lambda t: na.root(a, t, parts_of(t))),
                                  (2, lambda t: na.relu(a, t, x_rows(t, 8), parts_of(t))), (3, copy)], 8)

        def dense1_tensor(p):
            na = norm_a.begin("d1")

            def product(t):
                s, n = t.slot(2), parts_of(t)
                p.wait_ge(d1_copied.sem, d1_copied.base + t.n + 1)
                if t.past(4):
                    p.wait_ge(d1_ready.sem, d1_ready.base + t.n - 3)
                nc.tensor.matmul(banks[4 + t.slot(4)][0:n, :], ones3[0:3, 0:n], bias_parts[0:3, 0, :], start=True, stop=False)
                for g in range(G):
                    last = nc.tensor.matmul(banks[4 + t.slot(4)][0:n, g * P:(g + 1) * P], feat_a[:, s, g * P:g * P + n],
                                            W["wself"][:, :], start=False, stop=(g == G - 1))
                last.then_inc(d1_mm.sem, 1)

            run_steps(p, BLOCKS, [(2, lambda t: na.turn(p, t, d1_copied, parts_of(t))), (3, product)], 8)

        l0_in, l0_out = Ring(gathered_a, 64, 0), Ring(stored, 64, 0)
        mask_in0, mask_in1, mask_in2, mask_in3 = (Ring(mask_landed, 16, i) for i in range(4))

        def mask_load(sp, which, scanned, landed):
            def load(t):
                if t.past(4):
                    sp.wait_ge(scanned.sem, scanned.base + t.n - 3)
                    sp.nop(nofuse=True)
                sp.dma_start(mask[:, t.slot(4), :],
                             mask_line[which:which + 1, bass.ds(t.n * ROW, ROW)].to_broadcast([P, ROW])
                             ).then_inc(landed[t.slot(4)], 16)
            return load

        def masks_sync(sp, which, scanned, landed):
            run_steps(sp, CHUNKS, [(0, mask_load(sp, which, scanned, landed))])

        def stage(pool, t, slot_ap, table, done):
            nc.gpsimd.tensor_copy(slot_ap, slice_of(table, t, G)).then_inc(done.sem, 1)

        def scan(v, t, op, mask_sems, bank, dest, scanned, read_by):
            s = t.slot(2)
            v.wait_ge(mask_sems[t.slot(4)], mask_sems.base(t.slot(4)) + t.round(4) * 16 + 16)
            if t.past(2):
                v.wait_ge(read_by.sem, read_by.base + t.n - 1)
            if t.past(1):
                v.wait_ge(scanned.sem, scanned.base + t.n)
                begin = dest[:, 1 - s, ROW - 1:ROW]
            else:
                begin = 0.0
            v.tensor_tensor_scan(dest[:, s, :], mask[:, t.slot(4), :], bank, begin, ALU.mult, op).then_inc(scanned.sem, 1)

        def layer0_pool(pool, nmax, nrows):
            def stage_gather(t):
                s = t.slot(4)
                if t.past(4):
                    pool.wait_ge(l0_in[s], l0_in.base(s) + t.round(4) * 64)
                    pool.nop(nofuse=True)
                stage(pool, t, index[:, s, 0, :], dst_s_t, l0_staged)

            def gather(t):
                s = t.slot(4)
                pool.wait_ge(l0_staged.sem, l0_staged.base + t.n + 1)
                if t.past(4):
                    pool.wait_ge(norm_a.rows, norm_a.base + t.n - 3)
                pool.nop(nofuse=True)
                for g in range(G):
                    pool.indirect_dma_start(out=rows_a[:, s, g, 0:P], out_offset=None, in_=x,
                                            in_offset=bass.IndirectOffsetOnAxis(ap=index[:, s, 0, g:g + 1], axis=0),
                                            bounds_check=nmax, oob_is_err=False).then_inc(l0_in[s], 16)

            def stage_scatter(t):
                s = t.slot(4)
                if t.past(4):
                    pool.wait_ge(l0_out[s], l0_out.base(s) + t.round(4) * 64)
                    pool.nop(nofuse=True)
                stage(pool, t, index[:, s, 1, :], end_t[:, 0, :], l0_staged2)
                stage(pool, t, rows_o[:, s, :, P + 1], count_t[:, 0, :], l0_counts)

            def scatter(t):
                s = t.slot(4)
                pool.wait_ge(l0_staged2.sem, l0_staged2.base + t.n + 1)
                pool.wait_ge(l0_counts.sem, l0_counts.base + t.n + 1)
                pool.wait_ge(l0_ready.sem, l0_ready.base + t.n + 1)
                pool.nop(nofuse=True)
                for g in range(G):
                    pool.indirect_dma_start(out=state, out_offset=bass.IndirectOffsetOnAxis(ap=index[:, s, 1, g:g + 1], axis=0),
                                            in_=rows_o[:, s, g, :], in_offset=None, compute_op=ALU.add,
                                            bounds_check=nrows, oob_is_err=True).then_inc(l0_out[s], 16)

            norm_a.begin("l0")
            run_steps(pool, CHUNKS, [(1, gather), (0, stage_gather), (7, scatter), (6, stage_scatter)])
            for s in range(4):
                pool.wait_ge(l0_out[s], l0_out.base(s) + 64 * len(range(s, CHUNKS, 4)))

        def layer0_vector(v):
            na = norm_a.begin("l0")

            def stats(t):
                v.wait_ge(l0_in[t.slot(4)], l0_in.base(t.slot(4)) + t.round(4) * 64 + 64)
                na.moments(v, t, rows_a[:, t.slot(4)])
                na.spread(v, t)
                na.between(v, t)
                na.variance(v, t)

            def scale(t):
                na.inverse(v, t)
                na.shift(v, t)

            def maxima(t):
                v.wait_ge(na.turned, na.base + t.n + 1)
                scan(v, t, ALU.max, mask_in0, banks[t.slot(2)][:, :], feat_a, scanned0, l0_mm)

            run_steps(v, CHUNKS, [(0, stats), (1, scale), (2, maxima)])

        def layer0_scalar(a):
            na = norm_a.begin("l0")

            def copy(t):
                a.wait_ge(l0_mm.sem, l0_mm.base + t.n + 1)
                if t.past(4):
                    a.wait_ge(l0_out[t.slot(4)], l0_out.base(t.slot(4)) + t.round(4) * 64)
                nc.scalar.activation(rows_o[:, t.slot(4), :, 0:P],
                                     banks[4 + t.slot(2)][:, :].rearrange("p (g d) -> p g d", g=G),
                                     ACT.Copy).then_inc(l0_ready.sem, 1)

            run_steps(a, CHUNKS, [(0, lambda t: na.root(a, t)),
                                  (1, lambda t: na.relu(a, t, rows_a[:, t.slot(4)])), (3, copy)])

        def layer0_tensor(p):
            na = norm_a.begin("l0")

            def product(t):
                s = t.slot(2)
                p.wait_ge(scanned0.sem, scanned0.base + t.n + 1)
                if t.past(2):
                    p.wait_ge(l0_ready.sem, l0_ready.base + t.n - 1)
                for g in range(G):
                    last = nc.tensor.matmul(banks[4 + s][:, g * P:(g + 1) * P], feat_a[:, s, g * P:(g + 1) * P],
                                            W["wneigh"][:, :], start=True, stop=True)
                last.then_inc(l0_mm.sem, 1)

            run_steps(p, CHUNKS, [(1, lambda t: na.turn(p, t, scanned0)), (3, product)])

        len_small = sb("len_small", [P, 4, 2, G])
        square = sb("square", [P, G, P])
        leaky = feat_b4

        def dense2_sync(sp, slow):
            def load(t):
                n = parts_of(t)
                if t.past(8):
                    sp.wait_ge(d2_x3.sem, d2_x3.base + t.n - 7)
                    sp.nop(nofuse=True)
                sp.dma_start(rows_ab[0:n, t.slot(8)].rearrange("p g d -> p (g d)"),
                             state_blocks[bass.ds(t.n * P, n), :]).then_inc(dense_in[t.slot(8)], 16)

            def store_x3(t):
                n = parts_of(t)
                sp.wait_ge(d2_x3.sem, d2_x3.base + t.n + 1)
                sp.nop(nofuse=True)
                sp.dma_start(state3_blocks[bass.ds(t.n * P, n), :], xin[0:n, t.slot(4), :]).then_inc(dense_out[t.slot(4)], 16)

            def store_out(t):
                n = parts_of(t)
                sp.wait_ge(d2_ready.sem, d2_ready.base + t.n + 1)
                sp.nop(nofuse=True)
                sp.dma_start(out_blocks[bass.ds(t.n * P, n), :], final[0:n, t.slot(4), :]).then_inc(dense_out[t.slot(4)], 16)

            run_steps(sp, BLOCKS, [(0, load, 8), (8, store_x3, 0), (8, store_out, 0)], 8, CHUNKS, slow)
            for s in range(2):
                sp.wait_ge(l1_spilt[s], 16 * len(range(s, CHUNKS, 2)))
            for s in range(4):
                sp.wait_ge(dense_out[s], d2_base(16, s, 4) + 32 * len(range(s, BLOCKS, 4)))

        final = feat_cd

        def dense2_vector(v, slow):
            na = norm_a.begin("d2")

            def stats(t):
                v.wait_ge(dense_in[t.slot(8)], d2_base(16, t.slot(8), 8) + t.round(8) * 16 + 16)
                na.moments(v, t, rows_ab[:, t.slot(8)], parts_of(t))

            def leak(t):
                s, n = t.slot(2), parts_of(t)
                v.wait_ge(d2_fifth.sem, d2_fifth.base + t.n + 1)
                v.tensor_tensor(leaky[0:n, t.slot(4), :], leaky[0:n, t.slot(4), :], banks[2 + s][0:n, :],
                                ALU.max).then_inc(d2_leaky.sem, 1)

            def clamp(t):
                r, n = t.slot(4), parts_of(t)
                v.wait_ge(d2_root.sem, d2_root.base + t.n + 1)
                v.tensor_scalar(len_small[0:n, r, 1], len_small[0:n, r, 1], 1e-12, None, ALU.max).then_inc(d2_chain.sem, 1)

            def invert(t):
                r, n = t.slot(4), parts_of(t)
                v.wait_ge(d2_chain.sem, d2_chain.base + t.n + 1)
                v.reciprocal(len_small[0:n, r, 1], len_small[0:n, r, 1]).then_inc(d2_inv.sem, 1)

            def new_x(t):
                r, n = t.slot(4), parts_of(t)
                v.wait_ge(d2_inv.sem, d2_inv.base + t.n + 1)
                if t.past(4):
                    v.wait_ge(dense_out[r], d2_base(16, r, 4) + t.round(4) * 32)
                for g in range(G):
                    last = v.scalar_tensor_tensor(xin[0:n, r, g * P:(g + 1) * P], leaky[0:n, r, g * P:(g + 1) * P],
                                                  len_small[0:n, r, 1, g:g + 1], rows_ab[0:n, t.slot(8), g, 0:P],
                                                  ALU.mult, ALU.add)
                last.then_inc(d2_x3.sem, 1)

            parts = parts_of
            run_steps(v, BLOCKS, [(0, stats), (2, lambda t: na.inverse(v, t, parts(t))), (6, clamp), (4, leak),
                                  (2, lambda t: na.shift(v, t, parts(t))), (6, invert), (0, lambda t: na.spread(v, t, parts(t))),
                                  (2, lambda t: na.affine(v, t, rows_ab[:, t.slot(8)], d2_share, parts(t), D2_SHARE)),
                                  (6, new_x), (0, lambda t: na.between(v, t, parts(t))),
                                  (0, lambda t: na.variance(v, t, parts(t)))], 8, CHUNKS, slow)

        def dense2_pool(pool, slow):
            def final_x(t):
                r, n = t.slot(4), parts_of(t)
                pool.wait_ge(d2_x3.sem, d2_x3.base + t.n + 1)
                pool.nop(nofuse=True)
                nc.gpsimd.tensor_tensor(final[0:n, r, :], xin[0:n, r, :], quiet[0:n, :], ALU.add).then_inc(d2_ready.sem, 1)

            run_steps(pool, BLOCKS, [(9, final_x)], 8, CHUNKS, slow)

        def dense2_scalar(a, slow):
            na = norm_a.begin("d2")

            def copy(t):
                s, n = t.slot(2), parts_of(t)
                a.wait_ge(na.turned, na.base + t.n + 1)
                if t.past(2):
                    a.wait_ge(d2_mm.sem, d2_mm.base + t.n - 1)
                nc.scalar.activation(feat_a[:, s, :].rearrange("p (g d) -> p g d", g=G)[:, :, 0:n],
                                     banks[s][:, :].rearrange("p (g d) -> p g d", g=G)[:, :, 0:n],
                                     ACT.Relu).then_inc(d2_copied.sem, 1)

            def fifth(t):
                s, r, n = t.slot(2), t.slot(4), parts_of(t)
                a.wait_ge(d2_mm.sem, d2_mm.base + t.n + 1)
                if t.past(4):
                    a.wait_ge(d2_x3.sem, d2_x3.base + t.n - 3)
                nc.scalar.activation(leaky[0:n, r, :], banks[2 + s][0:n, :], ACT.Copy, scale=0.2).then_inc(d2_fifth.sem, 1)

            def squares(t):
                r, n = t.slot(4), parts_of(t)
                a.wait_ge(d2_leaky.sem, d2_leaky.base + t.n + 1)
                for g in range(G):
                    last = nc.scalar.activation(square[0:n, g, :], leaky[0:n, r, g * P:(g + 1) * P], ACT.Square,
                                                accum_out=len_small[0:n, r, 0, g:g + 1])
                last.then_inc(d2_norm.sem, 1)

            def length(t):
                r, n = t.slot(4), parts_of(t)
                a.wait_ge(d2_norm.sem, d2_norm.base + t.n + 1)
                nc.scalar.activation(len_small[0:n, r, 1], len_small[0:n, r, 0], ACT.Sqrt).then_inc(d2_root.sem, 1)

            run_steps(a, BLOCKS, [(1, lambda t: na.root(a, t, parts_of(t))), (4, fifth), (3, copy), (5, squares),
                                  (2, lambda t: na.relu(a, t, rows_ab[:, t.slot(8)], parts_of(t), D2_SHARE)), (5, length)], 8, CHUNKS, slow)

        def dense2_tensor(p, slow):
            na = norm_a.begin("d2")

            def product(t):
                s, n = t.slot(2), parts_of(t)
                p.wait_ge(d2_copied.sem, d2_copied.base + t.n + 1)
                if t.past(2):
                    p.wait_ge(d2_leaky.sem, d2_leaky.base + t.n - 1)
                for g in range(G):
                    last = nc.tensor.matmul(banks[2 + s][0:n, g * P:(g + 1) * P], feat_a[:, s, g * P:g * P + n],
                                            W["m1w"][:, :], start=True, stop=True)
                last.then_inc(d2_mm.sem, 1)

            run_steps(p, BLOCKS, [(2, lambda t: na.turn(p, t, d2_copied, parts_of(t), split=d2_share)), (3, product)], 8, CHUNKS, slow)

        l1_src_in, l1_dst_in, l1_spilt = sems("l1_src_in", 2), sems("l1_dst_in", 2), sems("l1_spilt", 2)
        ends_s, ends_d = rows_o[:, 0:2], rows_o[:, 2:4]
        TURNED_S, TURNED_D, PRODUCT = 5, 6, 4

        def layer1a_sync(sp):
            def spill(t):
                s = t.slot(2)
                sp.wait_ge(l1_dst_in[s], t.round(2) * 64 + 64)
                sp.nop(nofuse=True)
                sp.dma_start(dst_rows[bass.ds(t.n, 1)].rearrange("o p (g d) -> (o p) g d", g=G),
                             ends_d[:, s, :, 0:P]).then_inc(l1_spilt[s], 16)
            return [(1, 0, spill)]

        def layer1a_pool(pool, nmax):
            def gather_from(rows, k, table, staged, landed, norm, others):
                def gather(t):
                    s = t.slot(2)
                    if t.past(2):
                        pool.wait_ge(landed[s], t.round(2) * 64)
                        pool.nop(nofuse=True)
                    stage(pool, t, index[:, s, k, :], table, staged)
                    pool.wait_ge(staged.sem, staged.base + t.n + 1)
                    if t.past(2):
                        pool.wait_ge(norm.rows, norm.base + t.n - 1)
                        pool.wait_ge(l1_degs.sem, l1_degs.base + t.n - 1)
                        if others is not None:
                            pool.wait_ge(others[s], t.round(2) * 16)
                    pool.nop(nofuse=True)
                    for g in range(G):
                        pool.indirect_dma_start(out=rows[:, s, g, :], out_offset=None, in_=state[0:N, :],
                                                in_offset=bass.IndirectOffsetOnAxis(ap=index[:, s, k, g:g + 1], axis=0),
                                                bounds_check=nmax, oob_is_err=False).then_inc(landed[s], 16)
                return gather
            norm_src.begin("l1")
            norm_dst.begin("l1")
            return [(0, 0, gather_from(ends_s, 0, src_t, l1_staged, l1_src_in, norm_src, None)),
                    (1, 0, gather_from(ends_d, 1, dst_t, l1_staged_d, l1_dst_in, norm_dst, l1_spilt))]

        def bn_stats_of(v, t, ready):
            width = TAIL if t.last else ROW
            v.wait_ge(ready.sem, ready.base + t.n + 1)
            v.nop(nofuse=True)
            if t.last:
                v.bn_stats(bn_parts[:, t.n, :], hidden[:, t.n * ROW:t.n * ROW + width])
            else:
                v.bn_stats(bn_parts[:, bass.ds(t.n, 1), :].rearrange("p o s -> p (o s)"),
                           hidden[:, bass.ds(t.n * ROW, ROW)])

        def layer1a_vector(v):
            ns, nd = norm_src.begin("l1"), norm_dst.begin("l1")

            def stats_src(t):
                v.wait_ge(l1_src_in[t.slot(2)], t.round(2) * 64 + 64)
                ns.moments(v, t, ends_s[:, t.slot(2)])

            def stats_dst(t):
                s = t.slot(2)
                v.wait_ge(l1_dst_in[s], t.round(2) * 64 + 64)
                nd.moments(v, t, ends_d[:, s])
                v.tensor_copy(slice_of(deg_s_t, t, G), ends_s[:, s, :, P + 1])
                v.tensor_copy(slice_of(deg_d_t, t, G), ends_d[:, s, :, P + 1]).then_inc(l1_degs.sem, 1)
                ns.spread(v, t)

            def variance(t):
                nd.spread(v, t)
                ns.between(v, t)
                nd.between(v, t)
                ns.variance(v, t)
                nd.variance(v, t)

            def scale(t):
                ns.inverse(v, t)
                nd.inverse(v, t)
                ns.shift(v, t)
                nd.shift(v, t)

            return [(0, 0, stats_src), (1, 0, stats_dst), (2, 0, variance), (0, 1, scale),
                    (1, 3, lambda t: bn_stats_of(v, t, l1_hidden))]

        def layer1a_scalar(a):
            ns, nd = norm_src.begin("l1"), norm_dst.begin("l1")

            def root(t):
                ns.root(a, t)
                nd.root(a, t)

            def copy_src(t):
                if t.past(1):
                    a.wait_ge(l1_mm.sem, l1_mm.base + t.n)
                a.wait_ge(ns.turned, ns.base + t.n + 1)
                nc.scalar.activation(feat_ends[:, 0, :], banks[TURNED_S][:, :], ACT.Copy).then_inc(l1_copied.sem, 1)

            def copy_dst(t):
                a.wait_ge(nd.turned, nd.base + t.n + 1)
                nc.scalar.activation(feat_ends[:, 1, :], banks[TURNED_D][:, :], ACT.Copy).then_inc(l1_copied_d.sem, 1)

            def keep(t):
                a.wait_ge(l1_mm.sem, l1_mm.base + t.n + 1)
                a.nop(nofuse=True)
                nc.scalar.activation(slice_of(hidden, t, ROW), banks[PRODUCT][:, :], ACT.Identity,
                                     bias=cols[:, E1B:E1B + 1]).then_inc(l1_hidden.sem, 1)

            return [(3, 0, root), (1, 1, lambda t: ns.relu(a, t, ends_s[:, t.slot(2)])),
                    (2, 1, lambda t: nd.relu(a, t, ends_d[:, t.slot(2)])), (3, 1, copy_src), (0, 2, copy_dst), (0, 3, keep)]

        def layer1a_tensor(p):
            ns, nd = norm_src.begin("l1"), norm_dst.begin("l1")

            def product(t):
                p.wait_ge(l1_copied.sem, l1_copied.base + t.n + 1)
                p.wait_ge(l1_copied_d.sem, l1_copied_d.base + t.n + 1)
                if t.past(1):
                    p.wait_ge(l1_hidden.sem, l1_hidden.base + t.n)
                nc.tensor.matmul(banks[PRODUCT][:, :], W["e1s"][:, :], feat_ends[:, 0, :], start=True, stop=False)
                nc.tensor.matmul(banks[PRODUCT][:, :], W["e1d"][:, :], feat_ends[:, 1, :],
                                 start=False, stop=True).then_inc(l1_mm.sem, 1)

            return [(2, 1, lambda t: ns.turn(p, t, l1_copied)), (3, 1, lambda t: nd.turn(p, t, l1_copied_d)), (1, 2, product)]

        bn_sems = [[sem(f"bn{i}_{n}") for n in ("agg", "root", "chain")] for i in range(2)]
        bn_done = sems("bn_done", 2)

        def batch_norm_vector(v, which, gamma, beta):
            agg, root, chain = bn_sems[which]
            v.drain().then_inc(chain, 1)
            v.wait_ge(chain, 1)
            v.bn_aggr(bn_mv[:, :], bn_parts[:, :, :].rearrange("p c s -> p (c s)")).then_inc(agg, 1)
            v.wait_ge(root, 1)
            v.reciprocal(bn_sd[:, :], bn_sd[:, :]).then_inc(chain, 1)
            v.wait_ge(chain, 2)
            v.tensor_tensor(bn_scale[:, :], bn_sd[:, :], cols[:, gamma:gamma + 1], ALU.mult).then_inc(chain, 1)
            v.wait_ge(chain, 3)
            v.tensor_tensor(bn_tmp[:, :], bn_mv[:, 0:1], bn_scale[:, :], ALU.mult).then_inc(chain, 1)
            v.wait_ge(chain, 4)
            v.tensor_tensor(bn_shift[:, :], cols[:, beta:beta + 1], bn_tmp[:, :], ALU.subtract).then_inc(bn_done[which], 1)

        def batch_norm_scalar(a, which):
            agg, root, _ = bn_sems[which]
            a.wait_ge(agg, 1)
            nc.scalar.activation(bn_sd[:, :], bn_mv[:, 1:2], ACT.Sqrt, bias=eps_col[:, 0:1]).then_inc(root, 1)
            a.wait_ge(bn_done[which], 1)


        def layer1b_scalar(a):
            def act(t):
                if t.past(2):
                    a.wait_ge(l1b_mm.sem, l1b_mm.base + t.n - 1)
                a.nop(nofuse=True)
                nc.scalar.activation(feat_a[:, t.slot(2), :], slice_of(hidden, t, ROW), ACT.Relu,
                                     bias=bn_shift[:, 0:1], scale=bn_scale[:, 0:1]).then_inc(l1b_act.sem, 1)

            def keep(t):
                a.wait_ge(l1b_mm.sem, l1b_mm.base + t.n + 1)
                a.nop(nofuse=True)
                nc.scalar.activation(slice_of(hidden, t, ROW), banks[t.slot(2)][:, :], ACT.Identity,
                                     bias=cols[:, E2B:E2B + 1]).then_inc(l1b_hidden.sem, 1)

            run_steps(a, CHUNKS, [(0, act), (1, keep)])

        def layer1b_tensor(p):
            def product(t):
                s = t.slot(2)
                p.wait_ge(l1b_act.sem, l1b_act.base + t.n + 1)
                if t.past(2):
                    p.wait_ge(l1b_hidden.sem, l1b_hidden.base + t.n - 1)
                nc.tensor.matmul(banks[s][:, :], W["e2"][:, :], feat_a[:, s, :], start=True, stop=True).then_inc(l1b_mm.sem, 1)
            run_steps(p, CHUNKS, [(0, product)])

        def layer1b_vector(v):
            run_steps(v, CHUNKS, [(0, lambda t: bn_stats_of(v, t, l1b_hidden))])

        l1c_rows, l1c_spilt, l1c_out = Ring(rows_back, 16, 0), Ring(rows_spilt, 16, 0), Ring(stored, 64, 1)

        def row_load(sp, used, landed):
            def load(t):
                if t.past(4):
                    sp.wait_ge(used.sem, used.base + t.n - 3)
                    sp.nop(nofuse=True)
                sp.dma_start(xin[:, t.slot(4), :], dst_rows[bass.ds(t.n, 1)].rearrange("o p f -> (o p) f")
                             ).then_inc(landed[t.slot(4)], 16)
            return load

        def row_spill(sp, ready, spilt):
            def spill(t):
                sp.wait_ge(ready.sem, ready.base + t.n + 1)
                sp.nop(nofuse=True)
                sp.dma_start(dst_rows[bass.ds(t.n, 1)].rearrange("o p (g d) -> (o p) g d", g=G),
                             rows_o[:, t.slot(4), :, 0:P]).then_inc(spilt[t.slot(4)], 16)
            return spill

        def layer1c_sync(sp):
            run_steps(sp, CHUNKS, [(0, mask_load(sp, 1, scanned1, mask_in1)), (0, row_load(sp, l1c_ready, l1c_rows)),
                                   (3, row_spill(sp, l1c_ready, l1c_spilt))])
            for s in range(4):
                sp.wait_ge(l1c_spilt[s], l1c_spilt.base(s) + 16 * len(range(s, CHUNKS, 4)))

        def layer1c_scalar(a):
            def act(t):
                if t.past(2):
                    a.wait_ge(scanned1.sem, scanned1.base + t.n - 1)
                a.nop(nofuse=True)
                nc.scalar.activation(feat_a[:, t.slot(2), :], slice_of(hidden, t, ROW), ACT.Relu,
                                     bias=bn_shift[:, 0:1], scale=bn_scale[:, 0:1]).then_inc(l1c_act.sem, 1)
            run_steps(a, CHUNKS, [(0, act)])

        def layer1c_vector(v):
            def sums(t):
                v.wait_ge(l1c_act.sem, l1c_act.base + t.n + 1)
                scan(v, t, ALU.add, mask_in1, feat_a[:, t.slot(2), :], feat_b, scanned1, l1c_turned)

            def add(t):
                s = t.slot(4)
                v.wait_ge(l1c_turned.sem, l1c_turned.base + t.n + 1)
                v.wait_ge(l1c_rows[s], l1c_rows.base(s) + t.round(4) * 16 + 16)
                if t.past(4):
                    v.wait_ge(l1c_out[s], l1c_out.base(s) + t.round(4) * 64)
                    v.wait_ge(l1c_spilt[s], l1c_spilt.base(s) + t.round(4) * 16)
                v.tensor_tensor(rows_o[:, s, :, 0:P], banks[t.slot(2)][:, :].rearrange("p (g d) -> p g d", g=G),
                                x_rows(t), ALU.add).then_inc(l1c_ready.sem, 1)

            run_steps(v, CHUNKS, [(0, sums), (1, add)])

        def layer1c_tensor(p):
            def turn(t):
                s = t.slot(2)
                p.wait_ge(scanned1.sem, scanned1.base + t.n + 1)
                if t.past(2):
                    p.wait_ge(l1c_ready.sem, l1c_ready.base + t.n - 1)
                for g in range(G):
                    last = nc.tensor.transpose(banks[s][:, g * P:(g + 1) * P], feat_b[:, s, g * P:(g + 1) * P], ident[:, :])
                last.then_inc(l1c_turned.sem, 1)
            run_steps(p, CHUNKS, [(0, turn)])

        def layer1c_pool(pool, nmax):
            def stage_scatter(t):
                s = t.slot(4)
                if t.past(4):
                    pool.wait_ge(l1c_out[s], l1c_out.base(s) + t.round(4) * 64)
                    pool.nop(nofuse=True)
                stage(pool, t, index[:, s, 1, :], end_t[:, 1, :], l1c_staged)
                stage(pool, t, rows_o[:, s, :, P], count_t[:, 1, :], l1c_facts)
                stage(pool, t, rows_o[:, s, :, P + 1], deg_d_t, l1c_facts2)

            def scatter(t):
                s = t.slot(4)
                pool.wait_ge(l1c_staged.sem, l1c_staged.base + t.n + 1)
                pool.wait_ge(l1c_facts.sem, l1c_facts.base + t.n + 1)
                pool.wait_ge(l1c_facts2.sem, l1c_facts2.base + t.n + 1)
                pool.wait_ge(l1c_ready.sem, l1c_ready.base + t.n + 1)
                pool.nop(nofuse=True)
                for g in range(G):
                    pool.indirect_dma_start(out=state[0:N, :],
                                            out_offset=bass.IndirectOffsetOnAxis(ap=index[:, s, 1, g:g + 1], axis=0),
                                            in_=rows_o[:, s, g, :], in_offset=None,
                                            bounds_check=nmax, oob_is_err=False).then_inc(l1c_out[s], 16)
            run_steps(pool, CHUNKS, [(1, scatter), (0, stage_scatter)])
            for s in range(4):
                pool.wait_ge(l1c_out[s], l1c_out.base(s) + 64 * len(range(s, CHUNKS, 4)))

        l2_in, l2_spilt, l2_out = Ring(gathered_a, 64, 1), Ring(rows_spilt, 16, 1), Ring(stored, 64, 2)

        def l2_rows_base(slot):
            return 2 * 16 * len(range(slot, BLOCKS, 8))

        def layer2_sync(sp):
            def row_load8(t):
                if t.past(8):
                    sp.wait_ge(l2_ready.sem, l2_ready.base + t.n - 7)
                    sp.nop(nofuse=True)
                sp.dma_start(xin[:, t.slot(8), :], dst_rows[bass.ds(t.n, 1)].rearrange("o p f -> (o p) f")
                             ).then_inc(dense_in[t.slot(8)], 16)

            run_steps(sp, CHUNKS, [(1, mask_load(sp, 1, scanned2, mask_in2)), (0, row_load8, 8),
                                   (8, row_spill(sp, l2_ready, l2_spilt))], 8)
            for s in range(4):
                sp.wait_ge(l2_spilt[s], l2_spilt.base(s) + 16 * len(range(s, CHUNKS, 4)))

        def edge_pool(pool, nmax, source, width, gathered, staged, fact, facts_done, facts_used,
                      target, out_sems, ready, staged2, facts_lag, lag):
            def stage_gather(t):
                s = t.slot(4)
                if t.past(4):
                    pool.wait_ge(gathered[s], gathered.base(s) + t.round(4) * 64)
                    pool.nop(nofuse=True)
                stage(pool, t, index[:, s, 0, :], src_t, staged)

            def gather(t):
                s = t.slot(4)
                pool.wait_ge(staged.sem, staged.base + t.n + 1)
                if t.past(4):
                    pool.wait_ge(norm_a.rows, norm_a.base + t.n - 3)
                pool.nop(nofuse=True)
                for g in range(G):
                    pool.indirect_dma_start(out=rows_a[:, s, g, 0:width], out_offset=None, in_=source,
                                            in_offset=bass.IndirectOffsetOnAxis(ap=index[:, s, 0, g:g + 1], axis=0),
                                            bounds_check=nmax, oob_is_err=False).then_inc(gathered[s], 16)

            def stage_scatter(t):
                s = t.slot(4)
                if t.past(4):
                    pool.wait_ge(out_sems[s], out_sems.base(s) + t.round(4) * 64)
                    pool.nop(nofuse=True)
                stage(pool, t, index[:, s, 1, :], end_t[:, 1, :], staged2)

            def scatter(t):
                s = t.slot(4)
                pool.wait_ge(staged2.sem, staged2.base + t.n + 1)
                pool.wait_ge(ready.sem, ready.base + t.n + 1)
                pool.nop(nofuse=True)
                for g in range(G):
                    pool.indirect_dma_start(out=target, out_offset=bass.IndirectOffsetOnAxis(ap=index[:, s, 1, g:g + 1], axis=0),
                                            in_=rows_o[:, s, g, 0:P], in_offset=None,
                                            bounds_check=nmax, oob_is_err=False).then_inc(out_sems[s], 16)

            def factors(t):
                s = t.slot(4)
                if t.past(4):
                    pool.wait_ge(facts_used.sem, facts_used.base + t.n - 3)
                    pool.nop(nofuse=True)
                stage(pool, t, facts[:, s, 0, :], fact, facts_done)

            run_steps(pool, CHUNKS, [(1, gather), (0, stage_gather), (facts_lag, factors), (lag, scatter), (lag - 1, stage_scatter)])
            for s in range(4):
                pool.wait_ge(out_sems[s], out_sems.base(s) + 64 * len(range(s, CHUNKS, 4)))

        def layer2_pool(pool, nmax):
            norm_a.begin("l2")
            edge_pool(pool, nmax, state[0:N, :], XW, l2_in, l2_staged, norm_t, l2_facts, l2_scaled,
                      state3, l2_out, l2_ready, l2_staged2, 4, 10)

        both_ends, h_n = feat_b4[:, 2:4], feat_cd

        def layer2_vector(v):
            na, nb = norm_a.begin("l2"), norm_b.begin("l2")

            def stats(t):
                s, r = t.slot(4), t.slot(8)
                v.wait_ge(l2_in[s], l2_in.base(s) + t.round(4) * 64 + 64)
                na.moments(v, t, rows_a[:, s])
                v.wait_ge(dense_in[r], l2_rows_base(r) + t.round(8) * 16 + 16)
                nb.moments(v, t, x_rows(t, 8))
                na.spread(v, t)
                nb.spread(v, t)
                na.between(v, t)
                nb.between(v, t)

            def variance(t):
                nb.variance(v, t)
                na.variance(v, t, degree=rows_a[:, t.slot(4), :, P])

            def inverse(t):
                na.inverse(v, t)
                nb.inverse(v, t)

            def shift(t):
                na.shift(v, t)
                nb.shift(v, t)

            def sums(t):
                v.wait_ge(na.turned, na.base + t.n + 1)
                scan(v, t, ALU.add, mask_in2, banks[t.slot(2)][:, :], feat_a, scanned2, l2_mm)

            def times(t):
                s = t.slot(2)
                v.wait_ge(scanned2.sem, scanned2.base + t.n + 1)
                v.wait_ge(l2_copied.sem, l2_copied.base + t.n + 1)
                v.tensor_tensor(both_ends[:, s, :], feat_a[:, s, :], feat_b[:, s, :], ALU.mult).then_inc(l2_prod.sem, 1)

            def total(t):
                r = t.slot(4)
                v.wait_ge(l2_scaled.sem, l2_scaled.base + t.n + 1)
                v.tensor_tensor(h_n[:, r, :], banks[6 + t.slot(2)][:, :], h_n[:, r, :], ALU.add).then_inc(l2_sum.sem, 1)

            def leak(t):
                r = t.slot(4)
                v.wait_ge(l2_sum.sem, l2_sum.base + t.n + 1)
                v.scalar_tensor_tensor(h_n[:, r, :], h_n[:, r, :], 0.2, h_n[:, r, :],
                                       ALU.mult, ALU.max).then_inc(l2_leaky.sem, 1)

            def clamp(t):
                r = t.slot(4)
                v.wait_ge(l2_root.sem, l2_root.base + t.n + 1)
                v.tensor_scalar(len_small[:, r, 1], len_small[:, r, 1], 1e-12, None, ALU.max).then_inc(l2_chain.sem, 1)

            def invert(t):
                r = t.slot(4)
                v.wait_ge(l2_chain.sem, l2_chain.base + t.n + 1)
                v.reciprocal(len_small[:, r, 1], len_small[:, r, 1]).then_inc(l2_inv.sem, 1)

            def finish(t):
                r = t.slot(4)
                v.wait_ge(l2_inv.sem, l2_inv.base + t.n + 1)
                if t.past(4):
                    v.wait_ge(l2_out[r], l2_out.base(r) + t.round(4) * 64)
                    v.wait_ge(l2_spilt[r], l2_spilt.base(r) + t.round(4) * 16)
                for g in range(G):
                    last = v.scalar_tensor_tensor(rows_o[:, r, g, 0:P], h_n[:, r, g * P:(g + 1) * P],
                                                  len_small[:, r, 1, g:g + 1], x_rows(t, 8)[:, g, :], ALU.mult, ALU.add)
                last.then_inc(l2_ready.sem, 1)

            run_steps(v, CHUNKS, [(0, stats), (3, sums), (6, clamp), (0, variance), (3, times), (1, inverse),
                                  (4, total), (6, invert), (1, shift), (4, leak), (6, finish)], 8)

        def layer2_scalar(a):
            na, nb = norm_a.begin("l2"), norm_b.begin("l2")

            def root(t):
                na.root(a, t, degree=True)
                nb.root(a, t)

            def relu(t):
                na.relu(a, t, rows_a[:, t.slot(4)])
                nb.relu(a, t, x_rows(t, 8))

            def copy(t):
                s = t.slot(2)
                if t.past(2):
                    a.wait_ge(l2_prod.sem, l2_prod.base + t.n - 1)
                    a.wait_ge(l2_mm.sem, l2_mm.base + t.n - 1)
                a.wait_ge(nb.turned, nb.base + t.n + 1)
                nc.scalar.activation(feat_b[:, s, :], banks[2 + s][:, :], ACT.Copy).then_inc(l2_copied.sem, 1)

            def message(t):
                s, r = t.slot(2), t.slot(4)
                a.wait_ge(l2_mm.sem, l2_mm.base + t.n + 1)
                a.wait_ge(l2_facts.sem, l2_facts.base + t.n + 1)
                if t.past(4):
                    a.wait_ge(l2_ready.sem, l2_ready.base + t.n - 3)
                for g in range(G):
                    last = nc.scalar.activation(h_n[:, r, g * P:(g + 1) * P], banks[4 + s][:, g * P:(g + 1) * P],
                                                ACT.Copy, scale=facts[:, r, 0, g:g + 1])
                last.then_inc(l2_scaled.sem, 1)

            def squares(t):
                r = t.slot(4)
                a.wait_ge(l2_leaky.sem, l2_leaky.base + t.n + 1)
                for g in range(G):
                    last = nc.scalar.activation(square[:, g, :], h_n[:, r, g * P:(g + 1) * P], ACT.Square,
                                                accum_out=len_small[:, r, 0, g:g + 1])
                last.then_inc(l2_norm.sem, 1)

            def length(t):
                r = t.slot(4)
                a.wait_ge(l2_norm.sem, l2_norm.base + t.n + 1)
                nc.scalar.activation(len_small[:, r, 1], len_small[:, r, 0], ACT.Sqrt).then_inc(l2_root.sem, 1)

            run_steps(a, CHUNKS, [(1, root), (3, copy), (5, squares), (4, message), (5, length), (2, relu)], 8)

        def layer2_tensor(p):
            na, nb = norm_a.begin("l2"), norm_b.begin("l2")

            def turn(t):
                na.turn(p, t, scanned2)
                nb.turn(p, t, l2_copied)

            def product(t):
                s = t.slot(2)
                p.wait_ge(l2_prod.sem, l2_prod.base + t.n + 1)
                if t.past(2):
                    p.wait_ge(l2_sum.sem, l2_sum.base + t.n - 1)
                for g in range(G):
                    cut = slice(g * P, (g + 1) * P)
                    nc.tensor.matmul(banks[4 + s][:, cut], feat_a[:, s, cut], W["m1w"][:, :], start=True, stop=False)
                    nc.tensor.matmul(banks[4 + s][:, cut], both_ends[:, s, cut], W["m2w"][:, :], start=False, stop=True)
                    last = nc.tensor.matmul(banks[6 + s][:, cut], feat_b[:, s, cut], W["m1w"][:, :], start=True, stop=True)
                last.then_inc(l2_mm.sem, 1)

            run_steps(p, CHUNKS, [(3, product), (2, turn)], 8)

        l3_in, l3_rows, l3_out = Ring(gathered_a, 64, 2), Ring(rows_back, 16, 1), Ring(stored, 64, 3)

        def layer3_sync(sp):
            run_steps(sp, CHUNKS, [(0, mask_load(sp, 1, scanned3, mask_in3)), (0, row_load(sp, l3_ready, l3_rows))])

        def layer3_pool(pool, nmax):
            norm_a.begin("l3")
            edge_pool(pool, nmax, state3, P, l3_in, l3_staged, coef_t, l3_facts, l3_coef,
                      out, l3_out, l3_ready, l3_staged2, 1, 9)

        def layer3_vector(v):
            na = norm_a.begin("l3")

            def stats(t):
                s = t.slot(4)
                v.wait_ge(l3_in[s], l3_in.base(s) + t.round(4) * 64 + 64)
                na.moments(v, t, rows_a[:, s])
                na.spread(v, t)
                na.between(v, t)
                na.variance(v, t)

            def scale(t):
                na.inverse(v, t)
                na.shift(v, t)

            def weigh(t):
                s = t.slot(2)
                v.wait_ge(na.rows, na.base + t.n + 1)
                v.wait_ge(l3_facts.sem, l3_facts.base + t.n + 1)
                for g in range(G):
                    last = v.tensor_scalar(na.tile[:, s, g, :], na.tile[:, s, g, :], facts[:, t.slot(4), 0, g:g + 1], None, ALU.mult)
                last.then_inc(l3_coef.sem, 1)

            def sums(t):
                v.wait_ge(na.turned, na.base + t.n + 1)
                scan(v, t, ALU.add, mask_in3, banks[t.slot(2)][:, :], feat_a, scanned3, l3_mm1)

            def add(t):
                s = t.slot(4)
                v.wait_ge(l3_mm2.sem, l3_mm2.base + t.n + 1)
                v.wait_ge(l3_rows[s], l3_rows.base(s) + t.round(4) * 16 + 16)
                if t.past(4):
                    v.wait_ge(l3_out[s], l3_out.base(s) + t.round(4) * 64)
                v.tensor_tensor(rows_o[:, s, :, 0:P], banks[4 + t.slot(2)][:, :].rearrange("p (g d) -> p g d", g=G),
                                x_rows(t), ALU.add).then_inc(l3_ready.sem, 1)

            run_steps(v, CHUNKS, [(0, stats), (1, scale), (2, weigh), (3, sums), (5, add)])

        def layer3_scalar(a):
            na = norm_a.begin("l3")

            def act(t):
                s = t.slot(2)
                a.wait_ge(l3_mm1.sem, l3_mm1.base + t.n + 1)
                if t.past(2):
                    a.wait_ge(l3_mm2.sem, l3_mm2.base + t.n - 1)
                nc.scalar.activation(feat_b[:, s, :], banks[2 + s][:, :], ACT.Relu, bias=cols[:, C1B:C1B + 1]).then_inc(l3_act.sem, 1)

            run_steps(a, CHUNKS, [(0, lambda t: na.root(a, t)), (1, lambda t: na.relu(a, t, rows_a[:, t.slot(4)])), (3, act)])

        def layer3_tensor(p):
            na = norm_a.begin("l3")

            def first(t):
                s = t.slot(2)
                p.wait_ge(scanned3.sem, scanned3.base + t.n + 1)
                if t.past(2):
                    p.wait_ge(l3_act.sem, l3_act.base + t.n - 1)
                nc.tensor.matmul(banks[2 + s][:, :], W["c1w"][:, :], feat_a[:, s, :], start=True, stop=True).then_inc(l3_mm1.sem, 1)

            def second(t):
                s = t.slot(2)
                p.wait_ge(l3_act.sem, l3_act.base + t.n + 1)
                if t.past(2):
                    p.wait_ge(l3_ready.sem, l3_ready.base + t.n - 1)
                nc.tensor.matmul(banks[4 + s][:, :], ones3[0:3, :], bias_parts[0:3, 1, :], start=True, stop=False)
                for g in range(G):
                    last = nc.tensor.matmul(banks[4 + s][:, g * P:(g + 1) * P], feat_b[:, s, g * P:(g + 1) * P],
                                            W["c2w"][:, :], start=False, stop=(g == G - 1))
                last.then_inc(l3_mm2.sem, 1)

            run_steps(p, CHUNKS, [(4, second), (2, lambda t: na.turn(p, t, scanned3, ready=l3_coef)), (3, first)])

        def payload_pool(pool, emax):
            pool.wait_ge(pay_cleared, 1)
            for i in range(2):
                def gather(t, i=i):
                    s = t.slot(4)
                    if t.past(4):
                        pool.wait_ge(pay_slots[i][s], t.round(4) * 64)
                        pool.nop(nofuse=True)
                    stage(pool, t, index[:, s, i, :], idx_t[:, i, :], pay_staged[i])
                    pool.wait_ge(pay_staged[i].sem, t.n + 1)
                    if t.past(4):
                        pool.wait_ge(pay_taken[i], t.n - 3)
                    pool.nop(nofuse=True)
                    for g in range(G):
                        pool.indirect_dma_start(out=pay_in_rows[:, i, s, g, :], out_offset=None, in_=payload,
                                                in_offset=bass.IndirectOffsetOnAxis(ap=index[:, s, i, g:g + 1], axis=0),
                                                bounds_check=emax, oob_is_err=False).then_inc(pay_slots[i][s], 16)

                def take(t, i=i):
                    s = t.slot(4)
                    pool.wait_ge(pay_slots[i][s], t.round(4) * 64 + 64)
                    pool.nop(nofuse=True)
                    nc.gpsimd.tensor_copy(pay[:, i, bass.ds(t.n * G, G), :], pay_in_rows[:, i, s, :, :]).then_inc(pay_taken[i], 1)

                run_steps(pool, CHUNKS, [(0, gather), (3, take)])
            pool.wait_ge(pay_taken[0], CHUNKS)
            pool.wait_ge(pay_taken[1], CHUNKS)
            nc.gpsimd.tensor_copy(dst_s_t[:, :], pay[:, 0, :, 1])
            nc.gpsimd.tensor_copy(src_t[:, :], pay[:, 1, :, 0])
            nc.gpsimd.tensor_copy(weight_t[:, :], pay[:, 1, :, 2])
            nc.gpsimd.tensor_copy(dst_t[:, :], pay[:, 1, :, 1]).then_inc(tables_ready, 1)

        pay_in_rows = sb("pay_in_rows", [P, 2, 4, G, 4])
        pay_slots = [sems(f"pay_slot{i}_", 4) for i in range(2)]
        pay_staged, pay_taken = [Count(m, 0) for m in sems("pay_staged", 2)], sems("pay_taken", 2)

        @block.sync
        def _(sp):
            for n, a in (("wself", wself_t), ("wneigh", wneigh_t), ("e1s", e1_src_t), ("e1d", e1_dst_t),
                         ("e2", e2_t), ("m1w", m1), ("m2w", m2), ("c1w", c1), ("c2w", c2)):
                sp.dma_start(W[n][:, :], a).then_inc(consts_in, 16)
            for i, a in enumerate((e1_b, e1_g, e1_be, e2_b, e2_g, e2_be, c1_b)):
                sp.dma_start(cols[:, i:i + 1], a.rearrange("(p o) -> p o", o=1)).then_inc(consts_in, 16)
            for i, a in enumerate((bias0, c2_b)):
                for g in range(G):
                    sp.dma_start(bias_rows[0:1, i, g * P:(g + 1) * P],
                                 a.rearrange("(o p) -> o p", o=1)).then_inc(consts_in, 16)
            sp.wait_ge(keys_cleared, 1)
            for i, a in enumerate((src, dst)):
                sp.dma_start(keys[0:FULL, i, :], a[0:FULL * 2 * P].rearrange("(r f) -> r f", f=2 * P)).then_inc(keys_in, 16)
                if LEFT:
                    sp.dma_start(keys[FULL:FULL + 1, i, 0:LEFT],
                                 a[FULL * 2 * P:E].rearrange("(r f) -> r f", r=1)).then_inc(keys_in, 16)
            sp.dma_start(weights_in[0:FULL, :],
                         edge_weight[0:FULL * 2 * P].rearrange("(r f) -> r f", f=2 * P)).then_inc(keys_in, 16)
            if LEFT:
                sp.dma_start(weights_in[FULL:FULL + 1, 0:LEFT],
                             edge_weight[FULL * 2 * P:E].rearrange("(r f) -> r f", r=1)).then_inc(keys_in, 16)
            sp.wait_ge(consts_made, 1)
            spare = state[N:N + TILES * P, :].rearrange("(c p g) d -> c p (g d)", p=P, g=G)
            with sp.Fori(0, CHUNKS) as c:
                sp.dma_start(spare[bass.ds(c, 1)].rearrange("o p f -> (o p) f"), zero_rows[:, :]).then_inc(spare_out, 16)
            for i in range(2):
                sp.dma_start(key_line[i:i + 1, 0:1], minus1[0:1, :]).then_inc(keys_out, 16)
                sp.dma_start(key_line[i:i + 1, SORT + 1:SORT + 2], minus1[0:1, :]).then_inc(keys_out, 16)
                sp.dma_start(start_line[i:i + 1, 0:1], zero2[0:1, :]).then_inc(starts_out, 16)
            sp.wait_ge(pack_ready, 1)
            sp.dma_start(payload[0:FULL * 2 * P, :].rearrange("(r f) w -> r (f w)", f=2 * P),
                         pack[0:FULL, :, :].rearrange("p f w -> p (f w)")).then_inc(pack_out, 16)
            if LEFT:
                sp.dma_start(payload[FULL * 2 * P:E, :].rearrange("(r f) w -> r (f w)", r=1),
                             pack[FULL:FULL + 1, 0:LEFT, :].rearrange("p f w -> p (f w)")).then_inc(pack_out, 16)
            line_view = "(h q p) -> q h p"
            sp.wait_ge(key_ready, 1)
            for i in range(2):
                sp.dma_start(key_line[i, 1:SORT + 1].rearrange(line_view, h=2, q=P),
                             key_f[:, i, :].rearrange("q (h p) -> q h p", h=2)).then_inc(keys_out, 16)
            sp.wait_ge(keys_out, 16 * 6)
            for i in range(2):
                sp.dma_start(prev_f[:, i, :].rearrange("q (h p) -> q h p", h=2),
                             key_line[i, 0:SORT].rearrange(line_view, h=2, q=P)).then_inc(neighbours_in, 16)
                sp.dma_start(next_f[:, i, :].rearrange("q (h p) -> q h p", h=2),
                             key_line[i, 2:SORT + 2].rearrange(line_view, h=2, q=P)).then_inc(neighbours_in, 16)
            sp.wait_ge(mask_ready, 1)
            for i in range(2):
                sp.dma_start(mask_line[i, :].rearrange(line_view, h=2, q=P),
                             mask_b[:, i, :].rearrange("q (h p) -> q h p", h=2)).then_inc(mask_out, 16)
            sp.wait_ge(rows_max, 1)
            with nc.allow_non_contiguous_dma(reason="256 single values"):
                for i in range(2):
                    for h in range(2):
                        sp.dma_start(start_line[i, 1 + h * P:1 + (h + 1) * P].rearrange("(q o) -> q o", o=1),
                                     row_max[:, i, h:h + 1]).then_inc(starts_out, 16)
                sp.wait_ge(starts_out, 16 * 6)
                sp.dma_start(line[:, :], start_line[:, 0:2 * P]).then_inc(starts_in, 16)
                sp.wait_ge(before_made, 1)
                sp.dma_start(before_line, line2[:, :]).then_inc(before_out, 16)
                sp.wait_ge(before_out, 16)
                for i in range(2):
                    for h in range(2):
                        sp.dma_start(row_before[:, i, h:h + 1],
                                     before_line[i, h * P:(h + 1) * P].rearrange("(q o) -> q o", o=1)).then_inc(before_in, 16)
            sp.wait_ge(bias_ready, 1)
            for k in range(3):
                sp.dma_start(bias_parts[k:k + 1, :, :], bias_split[0:1, k]).then_inc(bias_in, 16)
            sp.wait_ge(bias_in, 48)
            sp.wait_ge(mask_out, 32)
            sp.wait_ge(pack_out, 32 if LEFT else 16)
            sp.wait_ge(spare_out, 16 * CHUNKS)
            phase_end(sp, "index")

            dense1_sync(sp)
            phase_end(sp, "dense1")
            masks_sync(sp, 0, scanned0, mask_in0)
            phase_end(sp, "layer0")
            dense2_sync(sp, layer1a_sync(sp))
            phase_end(sp, "layer1a")
            phase_end(sp, "layer1b")
            layer1c_sync(sp)
            phase_end(sp, "layer1c")
            layer2_sync(sp)
            phase_end(sp, "layer2")
            layer3_sync(sp)
            phase_end(sp, "layer3")

        @block.gpsimd
        def _(pool):
            g = nc.gpsimd
            g.memset(ident[:, :], 0.0).then_inc(ident_made, 1)
            pool.wait_ge(ident_made, 1)
            g.affine_select(out=ident[:, :], in_=ident[:, :], compare_op=ALU.not_equal, fill=1.0, base=0,
                            pattern=[[-1, P]], channel_multiplier=1).then_inc(ident_made, 1)
            g.iota(place[:, :], pattern=[[1, 2 * P]], base=0, channel_multiplier=2 * P).then_inc(idx_made, 1)
            g.iota(gray[:, :].rearrange("q (h p) -> q h p", h=2), pattern=[[P * P, 2], [1, P]], base=0,
                   channel_multiplier=P).then_inc(place_made, 1)
            phase_end(pool, "index")
            nmax, emax, rmax = pool.to_reg(N - 1), pool.to_reg(E - 1), pool.to_reg(N + TILES * P - 1)
            payload_pool(pool, emax)
            phase_end(pool, "dense1")
            layer0_pool(pool, nmax, rmax)
            phase_end(pool, "layer0")
            dense2_pool(pool, layer1a_pool(pool, nmax))
            phase_end(pool, "layer1a")
            phase_end(pool, "layer1b")
            layer1c_pool(pool, nmax)
            phase_end(pool, "layer1c")
            layer2_pool(pool, nmax)
            phase_end(pool, "layer2")
            layer3_pool(pool, nmax)
            phase_end(pool, "layer3")

        @block.vector
        def _(v):
            done = [0]

            def link(ins):
                done[0] += 1
                ins.then_inc(sorted_step, 1)
                v.wait_ge(sorted_step, done[0])

            v.memset(keys[:, :, :], PAD_KEY)
            v.memset(weights_in[:, :], 0.0).then_inc(keys_cleared, 1)
            v.memset(zero_rows[:, :], 0.0)
            v.memset(ones_row[:, :], 1.0)
            v.memset(ones3[:, :], 1.0)
            v.memset(minus1[:, :], -1.0)
            v.memset(zero2[:, :], 0.0)
            v.memset(eps_col[:, :], LN_EPS)
            v.memset(rows_ab[:, :, :, :], 0.0)
            v.memset(rows_o[:, :, :, :], 0.0)
            v.memset(pay_in_rows[:, :, :, :, :], 0.0)
            v.memset(pack[:, :, :], 0.0).then_inc(pay_cleared, 1)
            v.drain().then_inc(consts_made, 1)

            v.wait_ge(keys_in, 16 * (6 if LEFT else 3))
            v.wait_ge(consts_made, 1)
            v.tensor_copy(pack[:, :, 0], keys[:, 0, :])
            v.tensor_copy(pack[:, :, 1], keys[:, 1, :])
            v.tensor_copy(pack[:, :, 2], weights_in[:, :]).then_inc(pack_ready, 1)
            link(v.tensor_scalar(tmp_f[:, :, :], keys[:, :, :], float(HALF), float(LIFT), ALU.is_ge, ALU.mult))
            link(v.scalar_tensor_tensor(tmp_i[:, :, :], keys[:, :, :], 256.0, tmp_f[:, :, :], ALU.add, ALU.add))
            link(v.tensor_scalar(tmp_i[:, :, :], tmp_i[:, :, :], IDX_BITS, None, ALU.logical_shift_left))
            v.wait_ge(idx_made, 1)
            for i in range(2):
                ins = v.tensor_tensor(sort_a[:, i, :].bitcast(I32), tmp_i[:, i, :], place[:, :], ALU.bitwise_or)
            link(ins)
            v.wait_ge(place_made, 1)
            link(v.tensor_copy(place_f[:, :], gray[:, :]))
            link(v.tensor_scalar(place[:, :], gray[:, :], 1, None, ALU.logical_shift_left))
            here, there = sort_a, sort_b
            turns = 0
            for kind, k in STEPS:
                if kind == "flip":
                    if k == 1:
                        link(v.tensor_scalar(flip[:, :], gray[:, :], 30, -2 ** 31, ALU.logical_shift_left, ALU.bitwise_and))
                        link(v.tensor_tensor(gray[:, :], gray[:, :], place[:, :], ALU.bitwise_xor))
                    else:
                        link(v.tensor_scalar(flip[:, :], gray[:, :], 31 - k, -2 ** 31, ALU.logical_shift_left, ALU.bitwise_and))
                    for i in range(2):
                        ins = v.tensor_tensor(here[:, i, :].bitcast(I32), here[:, i, :].bitcast(I32), flip[:, :], ALU.bitwise_xor)
                    link(ins)
                elif kind == "turn":
                    turns += 1
                    v.wait_ge(copied_sort, turns)
                    here, there = there, here
                elif kind == "pair":
                    a = here[:, :, :].rearrange("q s (o two i) -> q (s o) two i", two=2, i=1 << k)
                    b = there[:, :, :].rearrange("q s (o two i) -> q (s o) two i", two=2, i=1 << k)
                    v.tensor_tensor(b[:, :, 0, :], a[:, :, 0, :], a[:, :, 1, :], ALU.max)
                    link(v.tensor_tensor(b[:, :, 1, :], a[:, :, 0, :], a[:, :, 1, :], ALU.min))
                    here, there = there, here
                sort_marks.append((kind, done[0], here is sort_a))
            result = here

            link(v.tensor_scalar(tmp_i[:, :, :], result[:, :, :].bitcast(I32), (1 << IDX_BITS) - 1, None, ALU.bitwise_and))
            link(v.tensor_copy(idx_f[:, :, :], tmp_i[:, :, :]))
            link(v.tensor_scalar(tmp_i[:, :, :], result[:, :, :].bitcast(I32), IDX_BITS, (1 << 17) - 1,
                                 ALU.logical_shift_right, ALU.bitwise_and))
            link(v.tensor_scalar(tmp_f[:, :, :], tmp_i[:, :, :], 65536.0, float(-LIFT), ALU.is_ge, ALU.mult))
            v.scalar_tensor_tensor(key_f[:, :, :], tmp_i[:, :, :], -256.0, tmp_f[:, :, :], ALU.add, ALU.add).then_inc(key_ready, 1)
            v.wait_ge(key_ready, 1)
            v.wait_ge(neighbours_in, 64)
            v.tensor_tensor(mask_b[:, :, :], key_f[:, :, :], prev_f[:, :, :], ALU.is_equal).then_inc(mask_ready, 1)
            link(v.tensor_tensor(first_f[:, :, :], key_f[:, :, :], prev_f[:, :, :], ALU.not_equal))
            for i in range(2):
                ins = v.tensor_tensor(first_f[:, i, :], first_f[:, i, :], place_f[:, :], ALU.mult)
            link(ins)
            for i in range(2):
                for h in range(2):
                    cut = slice(h * P, (h + 1) * P)
                    ins = v.tensor_tensor_scan(count_f[:, i, cut], first_f[:, i, cut], first_f[:, i, cut], 0.0, ALU.max, ALU.max)
            link(ins)
            v.tensor_copy(row_max[:, :, :], count_f[:, :, :].rearrange("q s (h p) -> q s h p", h=2)[:, :, :, P - 1]).then_inc(rows_max, 1)
            link(v.tensor_tensor(end_f[:, :, :], key_f[:, :, :], next_f[:, :, :], ALU.not_equal))
            link(v.tensor_scalar(tmp_f[:, :, :], key_f[:, :, :], float(N), None, ALU.is_lt))
            link(v.tensor_tensor(end_f[:, :, :], end_f[:, :, :], tmp_f[:, :, :], ALU.mult))
            link(v.tensor_scalar(prev_f[:, 0, :], place_f[:, :], float(N), None, ALU.add))
            v.memset(prev_f[:, 1, :], float(FAR))
            link(v.drain())
            link(v.tensor_tensor(next_f[:, :, :], key_f[:, :, :], prev_f[:, :, :], ALU.subtract))
            link(v.tensor_tensor(next_f[:, :, :], next_f[:, :, :], end_f[:, :, :], ALU.mult))
            link(v.tensor_tensor(end_f[:, :, :], next_f[:, :, :], prev_f[:, :, :], ALU.add))
            v.wait_ge(starts_in, 16)
            v.tensor_tensor_scan(line2[:, :], line[:, :], line[:, :], 0.0, ALU.max, ALU.max).then_inc(before_made, 1)
            v.wait_ge(before_in, 64)
            for i in range(2):
                for h in range(2):
                    cut = slice(h * P, (h + 1) * P)
                    ins = v.tensor_scalar(first_f[:, i, cut], count_f[:, i, cut], row_before[:, i, h:h + 1], -1.0, ALU.max, ALU.mult)
            link(ins)
            for i in range(2):
                ins = v.scalar_tensor_tensor(count_f[:, i, :], first_f[:, i, :], 1.0, place_f[:, :], ALU.add, ALU.add)
            ins.then_inc(fields_ready, 1)

            for i, (field, table) in enumerate(((idx_f, idx_t), (end_f, end_t), (count_f, count_t))):
                v.wait_ge(fields_turned, i + 1)
                v.tensor_copy(table[:, :, :].rearrange("p s t -> p (s t)"), banks[i][:, :]).then_inc(fields_taken, 1)
            v.wait_ge(consts_in, 16 * 24)
            v.wait_ge(consts_made, 1)
            v.tensor_scalar(relu_b[:, :], zero_rows[:, 0:P], cols[:, C1B:C1B + 1], 0.0, ALU.add, ALU.max).then_inc(quiet_col, 1)
            link(v.tensor_copy(bias_split[0:1, 0], bias_rows[0:1]))
            link(v.tensor_tensor(bias_left[0:1], bias_rows[0:1], bias_split[0:1, 0], ALU.subtract))
            link(v.tensor_copy(bias_split[0:1, 1], bias_left[0:1]))
            link(v.tensor_tensor(bias_left[0:1], bias_left[0:1], bias_split[0:1, 1], ALU.subtract))
            v.tensor_copy(bias_split[0:1, 2], bias_left[0:1]).then_inc(bias_ready, 1)
            v.wait_ge(quiet_done, 1)
            v.tensor_copy(quiet[:, :], banks[7][:, :])
            phase_end(v, "index")

            dense1_vector(v)
            phase_end(v, "dense1")
            layer0_vector(v)
            v.wait_ge(norm_rooted, 1)
            v.reciprocal(norm_t[:, :], norm_t[:, :])
            phase_end(v, "layer0")
            dense2_vector(v, layer1a_vector(v))
            batch_norm_vector(v, 0, E1G, E1BE)
            v.tensor_scalar(deg_s_t[:, :], deg_s_t[:, :], 1.0, None, ALU.max).then_inc(index_chain, 1)
            v.wait_ge(index_chain, 1)
            v.scalar_tensor_tensor(coef_t[:, :], deg_d_t[:, :], 1.0, deg_s_t[:, :], ALU.max, ALU.mult).then_inc(coef_made, 1)
            phase_end(v, "layer1a")
            layer1b_vector(v)
            batch_norm_vector(v, 1, E2G, E2BE)
            v.wait_ge(coef_rooted, 1)
            v.reciprocal(coef_t[:, :], coef_t[:, :]).then_inc(index_chain, 1)
            v.wait_ge(index_chain, 2)
            v.tensor_tensor(coef_t[:, :], coef_t[:, :], weight_t[:, :], ALU.mult)
            phase_end(v, "layer1b")
            layer1c_vector(v)
            phase_end(v, "layer1c")
            layer2_vector(v)
            phase_end(v, "layer2")
            layer3_vector(v)
            phase_end(v, "layer3")

        @block.scalar
        def _(a):
            turns = 0
            for kind, _, in_a in sort_marks:
                if kind == "turn":
                    turns += 1
                    a.wait_ge(turned_sort, turns)
                    target = sort_a if in_a else sort_b
                    nc.scalar.activation(target[:, :, :].rearrange("p s t -> p (s t)"), banks[turns % 2][:, :],
                                         ACT.Copy).then_inc(copied_sort, 1)
            phase_end(a, "index")
            dense1_scalar(a)
            phase_end(a, "dense1")
            nc.scalar.activation(norm_t[:, :], count_t[:, 1, 0:TILES], ACT.Sqrt).then_inc(norm_rooted, 1)
            layer0_scalar(a)
            phase_end(a, "layer0")
            dense2_scalar(a, layer1a_scalar(a))
            batch_norm_scalar(a, 0)
            a.wait_ge(coef_made, 1)
            nc.scalar.activation(coef_t[:, :], coef_t[:, :], ACT.Sqrt).then_inc(coef_rooted, 1)
            phase_end(a, "layer1a")
            layer1b_scalar(a)
            batch_norm_scalar(a, 1)
            phase_end(a, "layer1b")
            layer1c_scalar(a)
            phase_end(a, "layer1c")
            layer2_scalar(a)
            phase_end(a, "layer2")
            layer3_scalar(a)
            phase_end(a, "layer3")

        @block.tensor
        def _(p):
            p.wait_ge(ident_made, 2)
            turns = 0
            for kind, steps, in_a in sort_marks:
                if kind == "turn":
                    turns += 1
                    p.wait_ge(sorted_step, steps)
                    if turns > 2:
                        p.wait_ge(copied_sort, turns - 2)
                    origin = sort_b if in_a else sort_a
                    for j in range(4):
                        last = nc.tensor.transpose(banks[turns % 2][:, j * P:(j + 1) * P],
                                                   origin[:, j // 2, (j % 2) * P:(j % 2 + 1) * P], ident[:, :])
                    last.then_inc(turned_sort, 1)
            p.wait_ge(fields_ready, 1)
            for i, field in enumerate((idx_f, end_f, count_f)):
                for j in range(4):
                    last = nc.tensor.transpose(banks[i][:, j * P:(j + 1) * P],
                                               field[:, j // 2, (j % 2) * P:(j % 2 + 1) * P], ident[:, :])
                last.then_inc(fields_turned, 1)
            p.wait_ge(quiet_col, 1)
            nc.tensor.matmul(banks[7][:, :], ones_row[0:1, :], bias_rows[0:1, 1, :], start=True, stop=False)
            for j in range(G):
                last = nc.tensor.matmul(banks[7][:, j * P:(j + 1) * P], relu_b[:, :], W["c2w"][:, :], start=False, stop=(j == G - 1))
            last.then_inc(quiet_done, 1)
            phase_end(p, "index")
            dense1_tensor(p)
            phase_end(p, "dense1")
            layer0_tensor(p)
            phase_end(p, "layer0")
            dense2_tensor(p, layer1a_tensor(p))
            phase_end(p, "layer1a")
            layer1b_tensor(p)
            phase_end(p, "layer1b")
            layer1c_tensor(p)
            phase_end(p, "layer1c")
            layer2_tensor(p)
            phase_end(p, "layer2")
            layer3_tensor(p)
            phase_end(p, "layer3")


def kernel(**inputs):
    import numpy as _np
    import concourse.bacc as _bacc
    from concourse import mybir as _mybir
    from concourse.bass_utils import run_bass_kernel_spmd as _run

    i = {k: _np.asarray(v) for k, v in inputs.items()}
    D = i["x"].shape[1]
    laid = {
        "x": i["x"], "src": i["src"], "dst": i["dst"], "edge_weight": i["edge_weight"],
        "wself_t": i["L0_gnn_W"][:, :D].T, "wneigh_t": i["L0_gnn_W"][:, D:].T, "bias0": i["L0_gnn_b"],
        "e1_src_t": i["L1_gnn_W1"][:, :D].T, "e1_dst_t": i["L1_gnn_W1"][:, D:].T, "e1_b": i["L1_gnn_b1"],
        "e1_g": i["L1_gnn_g1"], "e1_be": i["L1_gnn_be1"],
        "e2_t": i["L1_gnn_W2"].T, "e2_b": i["L1_gnn_b2"], "e2_g": i["L1_gnn_g2"], "e2_be": i["L1_gnn_be2"],
        "m1": i["L2_gnn_W1"], "m2": i["L2_gnn_W2"],
        "c1": i["L3_gnn_W1"], "c1_b": i["L3_gnn_b1"], "c2": i["L3_gnn_W2"], "c2_b": i["L3_gnn_b2"],
    }
    nc = _bacc.Bacc("TRN2", target_bir_lowering=False, num_devices=1)
    arrays, args = {}, []
    for name, a in laid.items():
        a = _np.ascontiguousarray(a)
        arrays[f"in_{name}"] = a
        args.append(nc.dram_tensor(f"in_{name}", a.shape, _mybir.dt.from_np(a.dtype), kind="ExternalInput").ap())
    args.append(nc.dram_tensor("out_x", i["x"].shape, _mybir.dt.float32, kind="ExternalOutput").ap())
    build_gnn(nc, *args)
    r = _run(nc, [arrays], core_ids=[0])
    return r.results[0]["out_x"]
```
